# Optimizing a Trainium2 kernel written in Bass

```python
import numpy as np
import jax
import jax.numpy as jnp

def _softmax(x, axis=-1):
    return jax.nn.softmax(x, axis=axis)

def _gelu(x):
    return jax.nn.gelu(x, approximate=True)

def _silu(x):
    return jax.nn.silu(x)

def _sigmoid(x):
    return jax.nn.sigmoid(x)

def _layernorm(x, axis=-1, eps=1e-05):
    m = jnp.mean(x, axis=axis, keepdims=True)
    v = jnp.var(x, axis=axis, keepdims=True)
    return (x - m) / jnp.sqrt(v + eps)

def _scatter_add(tgt, idx, src, axis=0):
    return tgt.at[idx].add(src)

def _segment_sum(src, seg, n):
    return jax.ops.segment_sum(src, seg, n)
kernel_name = 'mk_adaln_d1_jaxref_r4_70e246'

def setup_inputs(seed: int=0):
    np.random.seed(seed)
    _w = jnp.asarray

    def _L0_attn_setup():
        import jax, jax.numpy as jnp
        import numpy as np
        N_HEADS = 16
        D_MODEL = 256
        SEQ_LEN = 512
        BATCH = 4
        key = jax.random.key(seed)
        k1, k2, k3 = jax.random.split(key, 3)
        std = 1.0 / np.sqrt(D_MODEL)
        x = jax.random.normal(k1, (BATCH, SEQ_LEN, D_MODEL), dtype=jnp.float32)
        w_qkv = std * jax.random.normal(k2, (D_MODEL, 3 * D_MODEL), dtype=jnp.float32)
        w_o = std * jax.random.normal(k3, (D_MODEL, D_MODEL), dtype=jnp.float32)
        return {'x': x, 'w_qkv': w_qkv, 'w_o': w_o}
    _L0_attn_in = _L0_attn_setup()

    def _L0_ffn_setup():
        import jax, jax.numpy as jnp
        import numpy as np
        N_EXPERTS = 8
        TOP_K = 2
        D_MODEL = 256
        HIDDEN = 1024
        ROUTED_H = 256
        BATCH, SEQ = (2, 1024)
        key = jax.random.key(seed)
        ks = jax.random.split(key, 8)
        std = 0.02
        return {'x': jax.random.normal(ks[0], (BATCH, SEQ, D_MODEL), dtype=jnp.float32), 'w12': std * jax.random.normal(ks[1], (N_EXPERTS, 2 * ROUTED_H, D_MODEL), dtype=jnp.float32), 'w3': std * jax.random.normal(ks[2], (N_EXPERTS, D_MODEL, ROUTED_H), dtype=jnp.float32), 'shared_w1': std * jax.random.normal(ks[3], (HIDDEN, D_MODEL), dtype=jnp.float32), 'shared_w2': std * jax.random.normal(ks[4], (HIDDEN, D_MODEL), dtype=jnp.float32), 'shared_w3': std * jax.random.normal(ks[5], (D_MODEL, HIDDEN), dtype=jnp.float32), 'router_w': std * jax.random.normal(ks[6], (N_EXPERTS, D_MODEL), dtype=jnp.float32), 'expert_bias': jnp.zeros((N_EXPERTS,), dtype=jnp.float32)}
    _L0_ffn_in = _L0_ffn_setup()
    _L0_c = _w((lambda *s: np.random.randn(*s).astype(np.float32) * 0.05)(8, 256))
    _L0_wmod = _w((lambda *s: np.random.randn(*s).astype(np.float32) * 0.05)(256, 6 * 256) * 256 ** (-0.5))
    _d = {'L0_attn_x': _L0_attn_in['x'], 'L0_attn_w_qkv': _L0_attn_in['w_qkv'], 'L0_attn_w_o': _L0_attn_in['w_o'], 'L0_ffn_w12': _L0_ffn_in['w12'], 'L0_ffn_w3': _L0_ffn_in['w3'], 'L0_ffn_shared_w1': _L0_ffn_in['shared_w1'], 'L0_ffn_shared_w2': _L0_ffn_in['shared_w2'], 'L0_ffn_shared_w3': _L0_ffn_in['shared_w3'], 'L0_ffn_router_w': _L0_ffn_in['router_w'], 'L0_ffn_expert_bias': _L0_ffn_in['expert_bias'], 'L0_c': _L0_c, 'L0_wmod': _L0_wmod}
    _x0 = _d['L0_attn_x']
    _d['L0_attn_x'] = jax.random.normal(jax.random.fold_in(jax.random.key(seed), 1), (8, 1024, 256), dtype=_x0.dtype)
    del _x0
    return _d

def reference(L0_attn_x, L0_attn_w_qkv, L0_attn_w_o, L0_ffn_w12, L0_ffn_w3, L0_ffn_shared_w1, L0_ffn_shared_w2, L0_ffn_shared_w3, L0_ffn_router_w, L0_ffn_expert_bias, L0_c, L0_wmod):

    def _L0_attn_ref(x, w_qkv, w_o):
        import jax, jax.numpy as jnp
        import numpy as np
        N_HEADS = 16
        D_MODEL = 256
        SEQ_LEN = 512
        BATCH = 4
        *lead, seq_len, d_model = x.shape
        head_dim = d_model // N_HEADS
        qkv = x @ w_qkv
        qkv = qkv.reshape(*qkv.shape[:-1], N_HEADS, 3 * head_dim)
        qkv = jnp.einsum('...Thd->...hTd', qkv)
        q, k, v = jnp.split(qkv, 3, axis=-1)
        scores = jnp.einsum('...hqd,...hkd->...hqk', q, k) / np.sqrt(d_model).astype(x.dtype)
        causal = jnp.tri(seq_len, dtype=bool)
        scores = jnp.where(causal, scores, jnp.asarray(-1e+30, dtype=scores.dtype))
        attn = jax.nn.softmax(scores, axis=-1)
        out = jnp.einsum('...hqk,...hkd->...qhd', attn, v)
        out = out.reshape(*out.shape[:-2], d_model)
        return out @ w_o

    def _L0_ffn_ref(x, w12, w3, shared_w1, shared_w2, shared_w3, router_w, expert_bias):
        import jax, jax.numpy as jnp
        import numpy as np
        N_EXPERTS = 8
        TOP_K = 2
        D_MODEL = 256
        HIDDEN = 1024
        ROUTED_H = 256
        BATCH, SEQ = (2, 1024)
        b, s, d = x.shape
        xf = x.reshape(-1, d)
        shared = jax.nn.silu(xf @ shared_w1.T) * (xf @ shared_w2.T) @ shared_w3.T
        scores = jax.nn.sigmoid(xf @ router_w.T)
        _, top_idx = jax.lax.top_k(scores + expert_bias, TOP_K)
        mask = jax.nn.one_hot(top_idx, N_EXPERTS, dtype=xf.dtype).sum(axis=-2)
        gates = scores * mask
        h12 = jnp.einsum('td,ehd->teh', xf, w12)
        h1, h2 = jnp.split(h12, 2, axis=-1)
        h = jax.nn.silu(h1) * h2 * gates[:, :, None]
        routed = jnp.einsum('teh,edh->td', h, w3)
        return (shared + routed).reshape(b, s, d)
    x = L0_attn_x
    mod = (_silu(L0_c) @ L0_wmod).reshape(L0_c.shape[0], 6, 1, -1)
    sa, ca, ga, sb, cb, gb = (mod[:, 0], mod[:, 1], mod[:, 2], mod[:, 3], mod[:, 4], mod[:, 5])
    ga = (2 * (ga >= 0) - 1) * jnp.maximum(jnp.abs(ga), 0.25)
    gb = (2 * (gb >= 0) - 1) * jnp.maximum(jnp.abs(gb), 0.25)
    h = _layernorm(x, axis=-1) * (1 + ca) + sa
    x = x + ga * _L0_attn_ref(h, L0_attn_w_qkv, L0_attn_w_o)
    h = _layernorm(x, axis=-1) * (1 + cb) + sb
    x = x + gb * _L0_ffn_ref(h, L0_ffn_w12, L0_ffn_w3, L0_ffn_shared_w1, L0_ffn_shared_w2, L0_ffn_shared_w3, L0_ffn_router_w, L0_ffn_expert_bias)
    return x

_drawn_inputs = setup_inputs


def setup_inputs(seed=0):
    import zlib

    import numpy as np

    out = dict(_drawn_inputs(seed))
    spreads = {'L0_ffn_expert_bias': (0.0, 0.8)}
    factors = {'L0_ffn_w12': 8.0,
     'L0_ffn_w3': 8.0,
     'L0_ffn_shared_w1': 6.794,
     'L0_ffn_shared_w2': 6.728,
     'L0_ffn_shared_w3': 6.709,
     'L0_ffn_router_w': 8.0}
    for name, (base, spread) in spreads.items():
        noise = np.random.default_rng([zlib.crc32(name.encode()), seed]).standard_normal(out[name].shape)
        drawn = base * np.exp(spread * noise) if base else spread * noise
        out[name] = jnp.asarray(drawn.astype(out[name].dtype))
    for name, factor in factors.items():
        out[name] = (out[name] * factor).astype(out[name].dtype)
    return out
```

```python
from contextlib import ExitStack

import concourse.bass as bass
from concourse import mybir

ALU = mybir.AluOpType
ACT = mybir.ActivationFunctionType
AX = mybir.AxisListType
F32 = mybir.dt.float32
BF16 = mybir.dt.bfloat16

P = 128
B, T, D = 8, 1024, 256
NH, HD = 16, 16
NT, NF = T // P, D // P
GH = 4
NG = NH // GH
VW = HD + 1
NE, RH, SH = 8, 256, 1024
NU = SH // RH + NE
NS = SH // RH
EPS = 1e-5
SCALE = 1.0 / 16.0
NEG = -1e30

Q_PART = (0, 0, 1, 0, 1, 2)
K_PART = (0, 1, 0, 2, 1, 0)
KS = HD * len(Q_PART)
SHIFT = 2

CHUNKS = []
for q0, nq, order in ((0, 512, (0, 1, 3, 2)), (512, 256, (0, 1, 2, 3, 4, 5)), (768, 256, (0, 1, 2, 3, 4, 5, 6, 7))):
    at, pieces = 0, []
    for kt in order:
        first = max(0, kt * P - q0)
        pieces.append((kt, first, nq - first, at))
        at += nq - first
    CHUNKS.append((q0, nq, pieces, at))
PTW = max(c[3] for c in CHUNKS)
NC = len(CHUNKS)
STEPS = NG * NC
UNITS = 2 * GH
DIAG = (((0, 512, 3), (896, 512, 1)), ((1024, 256, 2),), ((1536, 256, 2),))

MAXCH = [(qt, 0, (qt + 1) * P, True, qt) for qt in range(4)]
for qt in range(4, NT):
    MAXCH += [(qt, 0, 512, False, NT + qt - 4), (qt, 512, (qt + 1) * P - 512, True, qt)]
NM = len(MAXCH)
S1_UNITS = 20

ST_LN1, ST_QK, ST_V, ST_ATT = 0, NF, NF + NG, NF + NG + 2
ST_OT = ST_ATT + STEPS * UNITS
ST_OP = ST_OT + NF
ST_LN2 = ST_OP + 2
ST_FFN = ST_LN2 + NF
ST_USES = ST_FFN + NU * 4
S1_FFN = NG * GH * NM
S1_USES = S1_FFN + NU * NT
MISC = ["max0", "out0", "max1", "out1", "out2", "out3", "max2", "out4", "out5", "out6", "max3",
        "out7", "out8", "out9", "out10", "out11", "router"]
MISC_AT = {name: i for i, name in enumerate(MISC)}
MISC_USES = len(MISC)
MASKS = sum(len(d) for d in DIAG) * GH * NG
DVE_STEPS = 56
POOL_SET = 8 + NE
DVE_SETUP = 8


def adaln_layer(nc, x, w_qk, w_v, w_o, ffn_w, router_w, bias, c_t, w_mod, out):
    assert ST_USES % 2 == 0 and S1_USES % 2 == 0 and STEPS % 2 == 0
    gates_dram = nc.dram_tensor("gates", [B, 2 * D], F32).ap()
    x_v = x.rearrange("b (t p) d -> b p t d", p=P)
    out_v = out.rearrange("b (t p) d -> b p t d", p=P)

    with ExitStack() as ctx:
        def sb(name, shape, dt):
            return ctx.enter_context(nc.sbuf_tensor(name, shape, dt))

        def psum(name, shape, dt):
            return ctx.enter_context(nc.psum_tensor(name, shape, dt))

        def sem(name):
            return ctx.enter_context(nc.semaphore(name))

        probs = sb("probs", [P, 2, GH * PTW], F32)
        q_stack = sb("q_stack", [P, NG, GH, T], BF16)
        k_stack = sb("k_stack", [P, NG, GH, T], BF16)
        x_sb = sb("x_sb", [P, NT, D], F32)
        norm = sb("norm", [P, NT, D], F32)
        feat = sb("feat", [P, NF, T], F32)
        v_sb = sb("v_sb", [P, NT, NH * VW + 16], F32)
        o_tok = sb("o_tok", [P, NT, D], F32)
        small = sb("small", [P, 1024], F32)
        wqk_sb = sb("wqk_sb", [P, NG, NF, P], F32)
        wv_sb = sb("wv_sb", [P, NF, D], F32)
        wo_sb = sb("wo_sb", [P, NF, D], F32)
        rw_sb = sb("rw_sb", [P, NF, NE], F32)
        ffn_sb = sb("ffn_sb", [P, 2, NF * 2 * RH + 2 * D], F32)
        gates = sb("gates_sb", [P, 2, D], F32)
        mask = sb("mask", [P, 512], BF16)
        junk = sb("junk", [P, 2, 512], BF16)
        ident = sb("ident", [P, P], F32)
        ident_b = sb("ident_b", [P, P], BF16)
        max_part = sb("max_part", [P, GH, NT + 4], F32)
        max_bf = sb("max_bf", [P, NT, SHIFT, GH], BF16)
        l_inv = sb("l_inv", [P, 4 * GH], F32)
        stats = sb("stats", [P, NT, 6], F32)
        mean_var = sb("mean_var", [P, NT, 2], F32)
        rstd = sb("rstd", [P, 3, NT], F32)
        mod_t = sb("mod_t", [P, B, 8], F32)
        mod_col = sb("mod_col", [P, 8], F32)
        bias_sb = sb("bias_sb", [P, NE], F32)
        desc = sb("desc", [P, NE], F32)
        score = sb("score", [P, NT, NE], F32)
        choice = sb("choice", [P, NT, NE], F32)
        hot = sb("hot", [P, 2, NT, NE], F32)
        peak = sb("peak", [P, NT], F32)
        gate = sb("gate", [P, NU, NT], F32)
        eps = sb("eps", [P, 1], F32)

        flat = probs[:, :, :].rearrange("p a n -> p (a n)")
        wmod_sb = flat[:, 0:NF * 6 * D].rearrange("p (f n) -> p f n", f=NF)
        mod_sb = flat[0:B, 4096:4096 + 6 * D]
        guard = flat[0:B, 6144:6144 + 4 * D].rearrange("p (a m n) -> p a m n", a=2, m=2)
        ct_sb = flat[:, 8192:8192 + NF * B]
        silu_c = flat[:, 8448:8448 + NF * B].rearrange("p (f b) -> p f b", f=NF)
        parts = [probs[:, 0, g * 1536:(g + 1) * 1536].bitcast(BF16).rearrange("p (a n) -> p a n", a=3) for g in range(NG)]
        rest = [probs[:, 1, g * T:(g + 1) * T] for g in range(NG)]
        o_raw = small[:, 0:512]
        shift_rows = small[0:SHIFT * GH, 512:1024].bitcast(BF16)
        silu_h = small[:, :].rearrange("p (a n) -> p a n", a=2)
        hidden = o_tok[:, :, :].rearrange("p t d -> p (t d)").rearrange("p (s h n) -> p s h n", s=2, h=2)
        w_up = [ffn_sb[:, s, 0:NF * 2 * RH].rearrange("p (f n) -> p f n", f=NF) for s in range(2)]
        w_down = [ffn_sb[:, s, NF * 2 * RH:].rearrange("p (h n) -> p h n", h=2) for s in range(2)]

        st = [psum(f"st{i}", [P, 1024], F32) for i in range(2)]
        s1 = [psum(f"s1_{i}", [P, 512], F32) for i in range(2)]
        pv = psum("pv", [P, 512], F32)
        misc = psum("misc", [P, 512], F32)
        misc_b = misc[:, :].bitcast(BF16)

        weights_in = sem("weights_in")
        pool_set = sem("pool_set")
        x_in, gates_in, out_done = sem("x_in"), sem("gates_in"), sem("out_done")
        ffn_in = [sem(f"ffn_in{s}") for s in range(2)]
        stacked = [sem(f"stacked{g}") for g in range(NG)]
        shift_in = sem("shift_in")
        st_full, s1_full, pv_full, misc_full = sem("st_full"), sem("s1_full"), sem("pv_full"), sem("misc_full")
        s1_free, scaled = sem("s1_free"), sem("scaled")
        dve_step, waits_apart = sem("dve_step"), sem("waits_apart")
        var_ready, std_ready, norm_ready = sem("var_ready"), sem("std_ready"), sem("norm_ready")
        feat_ready, mod_ready = sem("feat_ready"), sem("mod_ready")
        part0_ready, rest_ready, part1_ready, part2_ready = sem("part0"), sem("rest"), sem("part1"), sem("part2")
        v_ready, max_ready, rows_ready = sem("v_ready"), sem("max_ready"), sem("rows_ready")
        exp_done, masked = sem("exp_done"), sem("masked")
        raw_ready, o_ready, x2_ready = sem("raw_ready"), sem("o_ready"), sem("x2_ready")
        score_ready, gate_ready, sum_zero = sem("score_ready"), sem("gate_ready"), sem("sum_zero")
        silu_ready, hidden_ready, out_ready = sem("silu"), sem("hidden_ready"), sem("out_ready")
        c_ready, guard_ready = sem("c_ready"), sem("guard_ready")

        block = ctx.enter_context(nc.Block())

        def apart(engine):
            engine.sem_inc(waits_apart, 1)

        def s1_quota(u):
            return min(GH * NM, GH * NM * u // S1_UNITS)

        @block.sync
        def _(sp):
            loads = ((ct_sb, c_t), (wmod_sb, w_mod), (wqk_sb[:, :, :, :], w_qk), (wv_sb[:, :, :], w_v),
                     (wo_sb[:, :, :], w_o), (rw_sb[:, :, :], router_w), (bias_sb[:, :], bias))
            for dst, src in loads:
                sp.dma_start(dst, src).then_inc(weights_in, 16)
            sp.wait_ge(guard_ready, 1)
            sp.dma_start(gates_dram, guard[:, 0, :, :]).then_inc(out_done, 16)
            sp.wait_ge(out_done, 16)
            with sp.Fori(0, B) as b:
                sp.wait_ge(out_ready, b + 1)
                sp.dma_start(x_sb[:, :, :], x_v[bass.ds(b, 1)].rearrange("o p t d -> (o p) t d")).then_inc(x_in, 16)
                sp.dma_start(gates[:, :, :].rearrange("p m n -> p (m n)"),
                             gates_dram[bass.ds(b, 1), :].to_broadcast([P, 2 * D])).then_inc(gates_in, 16)
                for g in range(NG):
                    sp.wait_ge(part2_ready, b * NG + g + 1)
                    for i in range(len(Q_PART)):
                        rows = slice(HD * i, HD * i + HD)
                        sp.dma_start(q_stack[rows, g, :, :], parts[g][0:64, Q_PART[i], :]).then_inc(stacked[g], 16)
                        sp.dma_start(k_stack[rows, g, :, :], parts[g][64:128, K_PART[i], :]).then_inc(stacked[g], 16)
                for g in range(NG):
                    sp.wait_ge(rows_ready, b * NG + g + 1)
                    sp.dma_start(q_stack[KS:KS + SHIFT, g, :, :], shift_rows).then_inc(shift_in, 16)
                for s in range(2):
                    sp.dma_start(ffn_sb[:, s, :], ffn_w[s]).then_inc(ffn_in[s], 16)
                with sp.Fori(1, NU // 2) as up:
                    for s in range(2):
                        sp.wait_ge(s1_free, b * S1_USES + up * (2 * NT) + (4 + S1_FFN + (s - 1) * NT))
                        sp.dma_start(ffn_sb[:, s, :], ffn_w[bass.ds(up * 2 + s, 1)].rearrange("o p n -> (o p) n")).then_inc(ffn_in[s], 16)
                sp.wait_ge(out_ready, b + 2)
                sp.dma_start(out_v[bass.ds(b, 1)].rearrange("o p t d -> (o p) t d"), norm[:, :, :]).then_inc(out_done, 16)
            sp.wait_ge(out_done, 16 * (B + 1))

        @block.gpsimd
        def _(pool):
            gp = nc.gpsimd
            gp.memset(ident[:, :], 0.0).then_inc(pool_set, 1)
            gp.memset(mask[:, :], 0.0).then_inc(pool_set, 1)
            gp.memset(v_sb[:, :, :], 1.0).then_inc(pool_set, 1)
            gp.memset(gate[:, :, :], 1.0).then_inc(pool_set, 1)
            gp.memset(eps[:, :], EPS).then_inc(pool_set, 1)
            for e in range(NE):
                gp.memset(desc[:, e:e + 1], float(NE - e)).then_inc(pool_set, 1)
            pool.wait_ge(pool_set, 5 + NE)
            gp.affine_select(ident[:, :], ident[:, :], [[-1, P]], ALU.not_equal, 1.0, 0, 1).then_inc(pool_set, 1)
            gp.affine_select(mask[:, 384:512], mask[:, 384:512], [[-1, P]], ALU.is_ge, NEG, 0, 1).then_inc(pool_set, 1)
            pool.wait_ge(pool_set, 7 + NE)
            gp.tensor_copy(ident_b[:, :], ident[:, :]).then_inc(pool_set, 1)
            with pool.Fori(0, B) as b:
                for g in range(NG):
                    pool.wait_ge(part1_ready, b * NG + g + 1)
                    gp.tensor_tensor(parts[g][:, 2, :], rest[g], parts[g][:, 1, :], ALU.subtract).then_inc(part2_ready, 1)
                for n in range(STEPS):
                    c = n % NC
                    for j in range(GH):
                        pool.wait_ge(exp_done, b * STEPS * UNITS + n * UNITS + 2 * j + 2)
                        apart(pool)
                        row = probs[:, n % 2, j * PTW:(j + 1) * PTW]
                        for at, step, k in DIAG[c]:
                            v = row[:, at:at + step * (k - 1) + P].rearrange("p (m n) -> p m n", n=P)[:, 0::step // P, :]
                            gp.affine_select(v, v, [[0, k], [1, P]], ALU.is_ge, 0.0, 0, -1).then_inc(masked, 1)
                pool.wait_ge(st_full, b * ST_USES + ST_LN2 + NF)
                apart(pool)
                gp.memset(norm[:, :, :], 0.0).then_inc(sum_zero, 1)

        @block.scalar
        def _(act):
            sc = nc.scalar
            act.wait_ge(weights_in, 16 * 7)
            sc.activation(silu_c.rearrange("p f b -> p (f b)"), ct_sb, ACT.Silu).then_inc(c_ready, 1)
            act.wait_ge(pool_set, POOL_SET)

            def norm_std(b, k):
                act.wait_ge(var_ready, b * 2 + k + 1)
                sc.activation(rstd[:, 0, :], mean_var[:, :, 1], ACT.Sqrt, bias=eps[:, 0:1]).then_inc(std_ready, 1)

            def modulate(b, k):
                for f in range(NF):
                    u = (ST_LN1, ST_LN2)[k] + f
                    act.wait_ge(st_full, b * ST_USES + u + 1)
                    sc.activation(feat[:, f, :], st[u % 2][:, :], ACT.Identity, bias=mod_col[:, 4 * k + f:4 * k + f + 1],
                                  scale=mod_col[:, 4 * k + 2 + f:4 * k + 3 + f]).then_inc(feat_ready, 1)

            def shift_copy(b, g):
                act.wait_ge(misc_full, b * MISC_USES + MISC_AT[f"max{g}"] + 1)
                if g >= 1:
                    act.wait_ge(shift_in, (b * NG + g) * 16)
                sc.activation(shift_rows, misc_b[0:SHIFT * GH, :], ACT.Copy).then_inc(rows_ready, 1)

            def raw_copy(b, n):
                nq = CHUNKS[n % NC][1]
                act.wait_ge(pv_full, b * STEPS + n + 1)
                if n >= 1:
                    act.wait_ge(misc_full, b * MISC_USES + MISC_AT[f"out{n - 1}"] + 1)
                sc.activation(o_raw[:, 0:nq], pv[:, 0:nq], ACT.Copy).then_inc(raw_ready, 1)

            def exps(b, n, u):
                c, j, t = n % NC, u // 2, u % 2
                w = (1024, CHUNKS[c][3] - 1024)[t]
                use = ST_ATT + n * UNITS + u
                act.wait_ge(st_full, b * ST_USES + use + 1)
                at = j * PTW + 1024 * t
                sc.activation(probs[:, n % 2, at:at + w], st[use % 2][:, 0:w], ACT.Exp, scale=SCALE).then_inc(exp_done, 1)

            with act.Fori(0, B) as b:
                norm_std(b, 0)
                act.wait_ge(mod_ready, b + 4)
                modulate(b, 0)
                for i in range(NG + 1):
                    if i < NG:
                        use = ST_QK + i
                        act.wait_ge(st_full, b * ST_USES + use + 1)
                        sc.activation(parts[i][:, 0, :], st[use % 2][:, :], ACT.Copy).then_inc(part0_ready, 1)
                    if i >= 1:
                        act.wait_ge(rest_ready, b * NG + i)
                        sc.activation(parts[i - 1][:, 1, :], rest[i - 1], ACT.Copy).then_inc(part1_ready, 1)
                shift_copy(b, 0)
                for g in range(NG):
                    act.wait_ge(stacked[g], (b + 1) * 16 * 2 * len(Q_PART))
                for n in range(STEPS):
                    if n >= 2:
                        act.wait_ge(pv_full, b * STEPS + n - 1)
                    for u in range(UNITS):
                        exps(b, n, u)
                    if n >= 1:
                        raw_copy(b, n - 1)
                    if n % NC == NC - 1 and n // NC + 1 < NG:
                        shift_copy(b, n // NC + 1)
                raw_copy(b, STEPS - 1)
                for f in range(NF):
                    use = ST_OT + f
                    act.wait_ge(st_full, b * ST_USES + use + 1)
                    sc.activation(feat[:, f, :], st[use % 2][:, :], ACT.Copy).then_inc(feat_ready, 1)
                norm_std(b, 1)
                modulate(b, 1)
                act.wait_ge(misc_full, b * MISC_USES + MISC_AT["router"] + 1)
                sc.activation(score[:, :, :].rearrange("p t e -> p (t e)"), misc[:, 0:NT * NE], ACT.Sigmoid).then_inc(score_ready, 1)
                with act.Fori(0, NU) as u:
                    for k in range(4):
                        act.wait_ge(st_full, b * ST_USES + u * 4 + (ST_FFN + k + 1))
                        sc.activation(silu_h[:, k % 2, :], st[(ST_FFN + k) % 2][:, 0:512], ACT.Silu).then_inc(silu_ready, 1)

        @block.vector
        def _(dve):
            vec = nc.vector
            count = [0, 0]

            def chain(ins, base):
                count[0] += 1
                ins.then_inc(dve_step, 1)
                dve.wait_ge(dve_step, base + count[0])

            for s in (out_ready, hidden_ready, score_ready, raw_ready):
                dve.sem_inc(s, 1)
            vec.memset(k_stack[KS:KS + SHIFT, :, :, :], 1.0).then_inc(dve_step, 1)
            count[0] += 1
            for k in range(3):
                dve.wait_ge(s1_full, k + 1)
                vec.tensor_copy(mod_sb[:, k * 512:(k + 1) * 512], s1[k % 2][0:B, :]).then_inc(s1_free, 1)
            dve.wait_ge(s1_free, 3)
            for m, idx in ((0, 2), (1, 5)):
                g = mod_sb[:, idx * D:(idx + 1) * D]
                chain(vec.tensor_scalar(guard[:, 0, m, :], g, 0.0, 2.0, ALU.is_ge, ALU.mult), 0)
                vec.scalar_tensor_tensor(guard[:, 1, m, :], g, -1.0, g, ALU.mult, ALU.max).then_inc(dve_step, 1)
                count[0] += 1
                chain(vec.tensor_scalar(guard[:, 0, m, :], guard[:, 0, m, :], -1.0, None, ALU.add), 0)
                ins = vec.scalar_tensor_tensor(guard[:, 0, m, :], guard[:, 1, m, :], 0.25, guard[:, 0, m, :], ALU.max, ALU.mult)
                if m == 0:
                    chain(ins, 0)
                else:
                    ins.then_inc(guard_ready, 1)
            dve.wait_ge(s1_full, 4)
            mt = mod_t[:, :, :].rearrange("p b k -> p k b")
            ps = s1[1][:, 0:8 * B].rearrange("p (k b) -> p k b", k=8)
            for i, add, done in ((0, 0.0, mod_ready), (2, 1.0, mod_ready), (4, 0.0, mod_ready), (6, 1.0, s1_free)):
                vec.tensor_scalar(mt[:, i:i + 2, :], ps[:, i:i + 2, :], add, None, ALU.add).then_inc(done, 1)
            dve.wait_ge(s1_free, 4)
            assert count[0] == DVE_SETUP, count[0]

            def layernorm(b, k, base):
                for t in range(NT):
                    vec.bn_stats(stats[:, t, :], x_sb[:, t, :]).then_inc(dve_step, 1)
                    count[0] += 1
                dve.wait_ge(dve_step, base + count[0])
                apart(dve)
                for t in range(NT):
                    ins = vec.bn_aggr(mean_var[:, t, :], stats[:, t, :])
                ins.then_inc(var_ready, 1)
                dve.wait_ge(std_ready, b * 2 + k + 1)
                chain(vec.reciprocal(rstd[:, 1, :], rstd[:, 0, :]), base)
                chain(vec.scalar_tensor_tensor(rstd[:, 2, :], mean_var[:, :, 0], -1.0, rstd[:, 1, :], ALU.mult, ALU.mult), base)
                for t in range(NT):
                    vec.tensor_scalar(norm[:, t, :], x_sb[:, t, :], rstd[:, 1, t:t + 1], rstd[:, 2, t:t + 1],
                                      ALU.mult, ALU.add).then_inc(norm_ready, 1)

            def maxima(b, g, i0, i1):
                for i in range(i0, i1):
                    j, (qt, k0, nk, masked_, col) = i // NM, MAXCH[i % NM]
                    use = g * GH * NM + i
                    dve.wait_ge(s1_full, b * S1_USES + 4 + use + 1)
                    dve.wait_ge(s1_free, b * S1_USES + 4 + use - 1)
                    to = max_part[:, j, col:col + 1]
                    if masked_:
                        apart(dve)
                        vec.tensor_tensor_reduce(junk[:, use % 2, 0:nk], s1[use % 2][:, 0:nk], mask[:, 512 - nk:512], 1.0, NEG,
                                                 ALU.add, ALU.max, to).then_inc(s1_free, 1)
                    else:
                        vec.tensor_reduce(to, s1[use % 2][:, 0:nk], AX.X, ALU.max).then_inc(s1_free, 1)

            def shifts(b, g, base):
                dve.wait_ge(s1_free, b * S1_USES + 4 + (g + 1) * GH * NM)
                hi = max_part[:, :, 4:NT]
                chain(vec.tensor_tensor(hi, hi, max_part[:, :, NT:NT + 4], ALU.max), base)
                m = max_part[:, :, 0:NT]
                parts_of = [max_bf[:, :, a, :].rearrange("p t j -> p j t") for a in range(SHIFT)]
                chain(vec.tensor_scalar(parts_of[0], m, -1.0, None, ALU.mult), base)
                vec.scalar_tensor_tensor(parts_of[1], m, -1.0, parts_of[0], ALU.mult, ALU.subtract).then_inc(max_ready, 1)

            def normalise(b, n, base):
                c = n % NC
                q0, nq = CHUNKS[c][:2]
                k = nq // P * GH
                dve.wait_ge(misc_full, b * MISC_USES + MISC_AT[f"out{n}"] + 1)
                o = misc[:, 0:k * 32].rearrange("p (k n) -> p k n", k=k)
                chain(vec.reciprocal(l_inv[:, 0:k], o[:, :, HD]), base)
                h0 = n // NC * GH * HD
                to = o_tok[:, q0 // P:(q0 + nq) // P, h0:h0 + GH * HD].rearrange("p t (j d) -> p t j d", j=GH)
                vec.tensor_tensor(to, o[:, :, 0:HD].rearrange("p (t j) d -> p t j d", j=GH),
                                  l_inv[:, 0:k].rearrange("p (t j) -> p t j", j=GH).unsqueeze(3).to_broadcast([P, nq // P, GH, HD]),
                                  ALU.mult).then_inc(o_ready, 1)

            def hide(b, u, k):
                dve.wait_ge(silu_ready, b * NU * 4 + u * 4 + (k + 1))
                use = ST_FFN + k
                vec.tensor_tensor(hidden[:, k // 2, k % 2, :], silu_h[:, k % 2, :], st[use % 2][:, 512:1024], ALU.mult)\
                   .then_inc(hidden_ready, 1)

            def add_up(b, u, c):
                for t in range(4):
                    use = S1_FFN + c * 4 + t
                    dve.wait_ge(s1_full, b * S1_USES + u * NT + (4 + use + 1))
                    tile = c * 4 + t
                    vec.scalar_tensor_tensor(norm[:, tile, :], s1[use % 2][:, 0:D], gate[:, bass.ds(u, 1), tile],
                                             norm[:, tile, :], ALU.mult, ALU.add).then_inc(s1_free, 1)

            dve.wait_ge(pool_set, POOL_SET)
            with dve.Fori(0, B) as b:
                count[0] = 0
                base = b * DVE_STEPS + DVE_SETUP
                dve.wait_ge(x_in, (b + 1) * 16)
                vec.tensor_copy(mod_col[:, :], mod_t[:, bass.ds(b, 1), :].rearrange("p o k -> p (o k)")).then_inc(mod_ready, 1)
                dve.wait_ge(out_done, (b + 1) * 16)
                layernorm(b, 0, base)
                for g in range(NG):
                    use = ST_QK + g
                    dve.wait_ge(part0_ready, b * NG + g + 1)
                    vec.tensor_tensor(rest[g], st[use % 2][:, :], parts[g][:, 0, :], ALU.subtract).then_inc(rest_ready, 1)
                for h in range(2):
                    use = ST_V + h
                    dve.wait_ge(st_full, b * ST_USES + use + 1)
                    for t in range(4):
                        to = v_sb[:, 4 * h + t, 0:NH * VW].rearrange("p (h d) -> p h d", d=VW)[:, :, 0:HD]
                        vec.tensor_copy(to, st[use % 2][:, t * D:(t + 1) * D].rearrange("p (h d) -> p h d", d=HD)).then_inc(v_ready, 1)
                maxima(b, 0, 0, GH * NM)
                shifts(b, 0, base)
                for n in range(STEPS):
                    g, c = n // NC, n % NC
                    for u in range(UNITS):
                        if g + 1 < NG:
                            maxima(b, g + 1, s1_quota(c * UNITS + u), s1_quota(c * UNITS + u + 1))
                        if u == 2 and n >= 2:
                            normalise(b, n - 2, base)
                    if c == NC - 1 and g + 1 < NG:
                        shifts(b, g + 1, base)
                normalise(b, STEPS - 2, base)
                normalise(b, STEPS - 1, base)
                dve.wait_ge(gates_in, (b + 1) * 16)
                for h in range(2):
                    use = ST_OP + h
                    dve.wait_ge(st_full, b * ST_USES + use + 1)
                    y = o_tok[:, 4 * h:4 * h + 4, :]
                    vec.tensor_tensor(y, st[use % 2][:, :].rearrange("p (t d) -> p t d", d=D),
                                      gates[:, 0, :].unsqueeze(1).to_broadcast([P, 4, D]), ALU.mult).then_inc(scaled, 1)
                    dve.wait_ge(scaled, b * 2 + h + 1)
                    chain(vec.tensor_tensor(x_sb[:, 4 * h:4 * h + 4, :], x_sb[:, 4 * h:4 * h + 4, :], y, ALU.add), base)
                layernorm(b, 1, base)
                dve.wait_ge(score_ready, b + 2)

                def wide(a):
                    return a.unsqueeze(2).to_broadcast([P, NT, NE])

                chain(vec.tensor_tensor(choice[:, :, :], score[:, :, :], bias_sb[:, :].unsqueeze(1).to_broadcast([P, NT, NE]), ALU.add), base)
                for r in range(2):
                    chain(vec.tensor_reduce(peak[:, :], choice[:, :, :], AX.X, ALU.max), base)
                    chain(vec.tensor_tensor(hot[:, r, :, :], choice[:, :, :], wide(peak[:, :]), ALU.is_equal), base)
                    chain(vec.tensor_tensor(hot[:, r, :, :], hot[:, r, :, :], desc[:, :].unsqueeze(1).to_broadcast([P, NT, NE]), ALU.mult), base)
                    chain(vec.tensor_reduce(peak[:, :], hot[:, r, :, :], AX.X, ALU.max), base)
                    chain(vec.tensor_tensor(hot[:, r, :, :], hot[:, r, :, :], wide(peak[:, :]), ALU.is_equal), base)
                    if r == 0:
                        chain(vec.scalar_tensor_tensor(choice[:, :, :], hot[:, 0, :, :], NEG, choice[:, :, :], ALU.mult, ALU.add), base)
                chain(vec.tensor_tensor(hot[:, 0, :, :], hot[:, 0, :, :], hot[:, 1, :, :], ALU.add), base)
                vec.tensor_tensor(gate[:, NS:NU, :].rearrange("p e t -> p t e"), hot[:, 0, :, :], score[:, :, :], ALU.mult).then_inc(gate_ready, 1)
                dve.wait_ge(gate_ready, b + 1)
                dve.wait_ge(sum_zero, b + 1)
                hide(b, 0, 0)
                hide(b, 0, 1)
                with dve.Fori(0, NU - 1) as u:
                    hide(b, u, 2)
                    hide(b, u, 3)
                    add_up(b, u, 0)
                    hide(b, u + 1, 0)
                    hide(b, u + 1, 1)
                    add_up(b, u, 1)
                hide(b, NU - 1, 2)
                hide(b, NU - 1, 3)
                add_up(b, NU - 1, 0)
                add_up(b, NU - 1, 1)
                dve.wait_ge(s1_free, (b + 1) * S1_USES + 4)
                chain(vec.tensor_tensor(norm[:, :, :], norm[:, :, :], gates[:, 1, :].unsqueeze(1).to_broadcast([P, NT, D]), ALU.mult), base)
                vec.tensor_tensor(norm[:, :, :], norm[:, :, :], x_sb[:, :, :], ALU.add).then_inc(out_ready, 1)
                dve.wait_ge(out_ready, b + 2)
                assert count[0] == DVE_STEPS, count[0]

        @block.tensor
        def _(pe):
            mm = nc.tensor.matmul
            pe.wait_ge(c_ready, 1)
            pe.wait_ge(pool_set, POOL_SET)
            for k in range(3):
                if k >= 2:
                    pe.wait_ge(s1_free, k - 1)
                for f in range(NF):
                    last = mm(s1[k % 2][0:B, :], silu_c[:, f, :], wmod_sb[:, f, k * 512:(k + 1) * 512], start=(f == 0), stop=(f == NF - 1))
                last.then_inc(s1_full, 1)
            pe.wait_ge(s1_free, 3)
            for i, idx in enumerate((0, 1, 3, 4)):
                for f in range(NF):
                    k = 2 * i + f
                    last = nc.tensor.transpose(s1[1][:, k * B:(k + 1) * B], mod_sb[:, idx * D + f * P:idx * D + (f + 1) * P], ident[0:B, 0:B])
            last.then_inc(s1_full, 1)

            def st_use(b, use):
                old = use - 2
                if old < 0:
                    pe.wait_ge(hidden_ready, b * NU * 4 + 1)
                elif old < ST_QK:
                    pe.wait_ge(feat_ready, b * 3 * NF + old + 1)
                elif old < ST_V:
                    pe.wait_ge(rest_ready, b * NG + old - ST_QK + 1)
                elif old < ST_ATT:
                    pe.wait_ge(v_ready, b * NT + 4 * (old - ST_V) + 4)
                elif old < ST_OT:
                    pe.wait_ge(exp_done, b * STEPS * UNITS + old - ST_ATT + 1)
                elif old < ST_OP:
                    pe.wait_ge(feat_ready, b * 3 * NF + NF + old - ST_OT + 1)
                elif old < ST_LN2:
                    pe.wait_ge(scaled, b * 2 + old - ST_OP + 1)
                else:
                    pe.wait_ge(feat_ready, b * 3 * NF + 2 * NF + old - ST_LN2 + 1)
                return st[use % 2]

            def misc_use(b, name):
                before = MISC[MISC_AT[name] - 1]
                if name == MISC[0]:
                    pe.wait_ge(score_ready, b + 1)
                elif before.startswith("max"):
                    pe.wait_ge(rows_ready, b * NG + int(before[3:]) + 1)
                else:
                    pe.wait_ge(o_ready, b * STEPS + int(before[3:]) + 1)

            def turn(b, src, first, ready, need):
                for f in range(NF):
                    to = st_use(b, first + f)
                    for t in range(NT):
                        pe.wait_ge(ready, need(t))
                        last = nc.tensor.transpose(to[:, t * P:(t + 1) * P], src[:, t, f * P:(f + 1) * P], ident[:, :])
                    last.then_inc(st_full, 1)

            def max_rows(b, g, i0, i1):
                for i in range(i0, i1):
                    j, (qt, k0, nk, _, _) = i // NM, MAXCH[i % NM]
                    use = g * GH * NM + i
                    pe.wait_ge(s1_free, b * S1_USES + 4 + use - 1)
                    mm(s1[use % 2][:, 0:nk], q_stack[0:KS, g, j, qt * P:(qt + 1) * P], k_stack[0:KS, g, j, k0:k0 + nk],
                       start=True, stop=True).then_inc(s1_full, 1)

            def max_turn(b, g):
                pe.wait_ge(max_ready, b * NG + g + 1)
                misc_use(b, f"max{g}")
                for qt in range(NT):
                    last = nc.tensor.transpose(misc_b[0:SHIFT * GH, qt * P:(qt + 1) * P],
                                               max_bf[:, qt, :, :].rearrange("p a j -> p (a j)"), ident_b[:, :])
                last.then_inc(misc_full, 1)

            def scores(b, n, u):
                g, c, j, t = n // NC, n % NC, u // 2, u % 2
                q0, nq, pieces, _ = CHUNKS[c]
                to = st_use(b, ST_ATT + n * UNITS + u)
                for kt, first, w, at in pieces:
                    if at // 1024 == t:
                        last = mm(to[:, at % 1024:at % 1024 + w], k_stack[0:KS + SHIFT, g, j, kt * P:(kt + 1) * P],
                                  q_stack[0:KS + SHIFT, g, j, q0 + first:q0 + nq], start=True, stop=True)
                last.then_inc(st_full, 1)

            def values(b, n, k0, k1):
                g, c = n // NC, n % NC
                _, nq, pieces, _ = CHUNKS[c]
                tiles = sorted(pieces)
                if k0 == 0:
                    pe.wait_ge(exp_done, b * STEPS * UNITS + (n + 1) * UNITS)
                    pe.wait_ge(masked, b * MASKS + sum(len(DIAG[i % NC]) * GH for i in range(n + 1)))
                    pe.wait_ge(raw_ready, b * STEPS + n + 1)
                for kt, first, w, at in tiles[k0:k1]:
                    for j in range(GH):
                        h = (g * GH + j) * VW
                        last = mm(pv[32 * j:32 * j + 32, first:nq], v_sb[:, kt, h:h + 32],
                                  probs[:, n % 2, j * PTW + at:j * PTW + at + w], start=(kt == 0), stop=(kt == len(tiles) - 1))
                if k1 >= len(tiles):
                    last.then_inc(pv_full, 1)

            def turn_out(b, n):
                nq = CHUNKS[n % NC][1]
                pe.wait_ge(raw_ready, b * STEPS + n + 2)
                misc_use(b, f"out{n}")
                for t in range(nq // P):
                    last = nc.tensor.transpose(misc[:, t * P:(t + 1) * P], o_raw[:, t * P:(t + 1) * P], ident[:, :])
                last.then_inc(misc_full, 1)

            def up(b, u, c, s, first=False):
                for h in range(2):
                    k = 2 * c + h
                    use = ST_FFN + k
                    if first and k < 2:
                        st_use(b, use)
                    else:
                        pe.wait_ge(hidden_ready, b * NU * 4 + u * 4 + k)
                    for m in range(2):
                        for f in range(NF):
                            last = mm(st[use % 2][:, 512 * m:512 * m + 512], w_up[s][:, f, m * RH + h * P:m * RH + (h + 1) * P],
                                      feat[:, f, c * 512:(c + 1) * 512], start=(f == 0), stop=(f == NF - 1))
                    last.then_inc(st_full, 1)

            def down(b, u, c, s):
                pe.wait_ge(hidden_ready, b * NU * 4 + u * 4 + (2 * c + 3))
                for t in range(4):
                    use = S1_FFN + c * 4 + t
                    pe.wait_ge(s1_free, b * S1_USES + u * NT + (4 + use - 1))
                    for h in range(2):
                        last = mm(s1[use % 2][:, 0:D], hidden[:, c, h, t * P:(t + 1) * P], w_down[s][:, h, :], start=(h == 0), stop=(h == 1))
                    last.then_inc(s1_full, 1)

            with pe.Fori(0, B) as b:
                turn(b, norm, ST_LN1, norm_ready, lambda t: b * 2 * NT + t + 1)
                pe.wait_ge(feat_ready, b * 3 * NF + NF)
                for g in range(NG):
                    to = st_use(b, ST_QK + g)
                    for c in range(2):
                        for f in range(NF):
                            last = mm(to[:, c * 512:(c + 1) * 512], wqk_sb[:, g, f, :], feat[:, f, c * 512:(c + 1) * 512],
                                      start=(f == 0), stop=(f == NF - 1))
                    last.then_inc(st_full, 1)
                for h in range(2):
                    to = st_use(b, ST_V + h)
                    for t in range(4):
                        for f in range(NF):
                            last = mm(to[:, t * D:(t + 1) * D], feat[:, f, (4 * h + t) * P:(4 * h + t + 1) * P], wv_sb[:, f, :],
                                      start=(f == 0), stop=(f == NF - 1))
                    last.then_inc(st_full, 1)
                pe.wait_ge(stacked[0], (b + 1) * 16 * 2 * len(Q_PART))
                max_rows(b, 0, 0, GH * NM)
                max_turn(b, 0)
                pe.wait_ge(v_ready, (b + 1) * NT)
                for n in range(STEPS):
                    g, c = n // NC, n % NC
                    if c == 0:
                        pe.wait_ge(shift_in, (b * NG + g + 1) * 16)
                        if g + 1 < NG:
                            pe.wait_ge(stacked[g + 1], (b + 1) * 16 * 2 * len(Q_PART))
                    for u in range(UNITS):
                        scores(b, n, u)
                        if g + 1 < NG:
                            max_rows(b, g + 1, s1_quota(c * UNITS + u), s1_quota(c * UNITS + u + 1))
                        if u == 1 and n >= 2:
                            turn_out(b, n - 2)
                        if u >= 2 and n >= 1:
                            k = len(CHUNKS[(n - 1) % NC][2])
                            values(b, n - 1, k * (u - 2) // 6, k * (u - 1) // 6)
                    if c == NC - 1 and g + 1 < NG:
                        max_turn(b, g + 1)
                values(b, STEPS - 1, 0, NT)
                turn_out(b, STEPS - 2)
                turn_out(b, STEPS - 1)
                turn(b, o_tok, ST_OT, o_ready, lambda t: (b + 1) * STEPS)
                pe.wait_ge(feat_ready, b * 3 * NF + 2 * NF)
                for h in range(2):
                    to = st_use(b, ST_OP + h)
                    for t in range(4):
                        for f in range(NF):
                            last = mm(to[:, t * D:(t + 1) * D], feat[:, f, (4 * h + t) * P:(4 * h + t + 1) * P], wo_sb[:, f, :],
                                      start=(f == 0), stop=(f == NF - 1))
                    last.then_inc(st_full, 1)
                turn(b, norm, ST_LN2, norm_ready, lambda t: b * 2 * NT + NT + t + 1)
                pe.wait_ge(feat_ready, (b + 1) * 3 * NF)
                misc_use(b, "router")
                for t in range(NT):
                    for f in range(NF):
                        last = mm(misc[:, t * NE:(t + 1) * NE], feat[:, f, t * P:(t + 1) * P], rw_sb[:, f, :], start=(f == 0), stop=(f == NF - 1))
                last.then_inc(misc_full, 1)
                pe.wait_ge(ffn_in[0], (b * (NU // 2) + 1) * 16)
                up(b, 0, 0, 0, first=True)
                with pe.Fori(0, NU // 2 - 1) as pair:
                    for s in range(2):
                        u = pair * 2 + s
                        up(b, u, 1, s)
                        down(b, u, 0, s)
                        pe.wait_ge(ffn_in[1 - s], b * (NU // 2) * 16 + pair * 16 + (16 if s == 0 else 32))
                        up(b, u + 1, 0, 1 - s)
                        down(b, u, 1, s)
                u = NU - 2
                up(b, u, 1, 0)
                down(b, u, 0, 0)
                pe.wait_ge(ffn_in[1], (b + 1) * (NU // 2) * 16)
                up(b, u + 1, 0, 1)
                down(b, u, 1, 0)
                up(b, u + 1, 1, 1)
                down(b, u + 1, 0, 1)
                down(b, u + 1, 1, 1)


def kernel(**inputs):
    import numpy as np
    import concourse.bacc as bacc
    from concourse.bass_utils import run_bass_kernel_spmd

    a = {n[3:]: np.asarray(v) for n, v in inputs.items()}
    tight = np.ascontiguousarray
    qkv = a["attn_w_qkv"].reshape(NF, P, NG, GH, 3, HD)
    w_qk = tight(qkv[:, :, :, :, 0:2].transpose(1, 2, 0, 4, 5, 3)).reshape(P, NG, NF, P)
    w_v = tight(qkv[:, :, :, :, 2].transpose(1, 0, 2, 3, 4)).reshape(P, NF, D)
    w_o = tight(a["attn_w_o"].reshape(NF, P, D).transpose(1, 0, 2))

    def unit(w1, w2, w3):
        w_up = np.concatenate([w1, w2], 0).reshape(2 * RH, NF, P).transpose(2, 1, 0).reshape(P, -1)
        w_down = w3.reshape(D, 2, P).transpose(2, 1, 0).reshape(P, -1)
        return np.concatenate([w_up, w_down], 1)

    units = [unit(a["ffn_shared_w1"][h:h + RH], a["ffn_shared_w2"][h:h + RH], a["ffn_shared_w3"][:, h:h + RH]) for h in range(0, SH, RH)]
    units += [unit(a["ffn_w12"][e, :RH], a["ffn_w12"][e, RH:], a["ffn_w3"][e]) for e in range(NE)]
    arrays = {
        "x": tight(a["attn_x"]),
        "w_qk": w_qk, "w_v": w_v, "w_o": w_o,
        "ffn_w": tight(np.stack(units)),
        "router_w": tight(a["ffn_router_w"].reshape(NE, NF, P).transpose(2, 1, 0)),
        "bias": tight(np.broadcast_to(a["ffn_expert_bias"], (P, NE))),
        "c_t": tight(a["c"].reshape(B, NF, P).transpose(2, 1, 0)).reshape(P, NF * B),
        "w_mod": tight(a["wmod"].reshape(NF, P, 6 * D).transpose(1, 0, 2)),
    }
    nc = bacc.Bacc("TRN2", target_bir_lowering=False, num_devices=1)
    args = {n: nc.dram_tensor(n, v.shape, mybir.dt.from_np(v.dtype), kind="ExternalInput").ap() for n, v in arrays.items()}
    args["out"] = nc.dram_tensor("out", (B, T, D), F32, kind="ExternalOutput").ap()
    adaln_layer(nc, **args)
    r = run_bass_kernel_spmd(nc, [arrays], core_ids=[0])
    return r.results[0]["out"]
```

```python
from contextlib import ExitStack

import concourse.bass as bass
from concourse import mybir

ALU = mybir.AluOpType
ACT = mybir.ActivationFunctionType
AX = mybir.AxisListType
F32 = mybir.dt.float32
BF16 = mybir.dt.bfloat16
F16 = mybir.dt.float16

P = 128
B, T, D = 8, 1024, 256
NH, HD = 16, 16
NT, NF = T // P, D // P
GH = 4
NG = NH // GH
VW = HD + 1
NE, RH, SH = 8, 256, 1024
NU = SH // RH + NE
NS = SH // RH
EPS = 1e-5
SCALE = 1.0 / 16.0
NEG = -1e30

Q_PART = (0, 0, 1, 0, 1, 2)
K_PART = (0, 1, 0, 2, 1, 0)
KS = HD * len(Q_PART)
SHIFT = 2

CHUNKS = []
for q0, nq, order in ((0, 512, (0, 1, 3, 2)), (512, 256, (0, 1, 2, 3, 4, 5)), (768, 256, (0, 1, 2, 3, 4, 5, 6, 7))):
    at, pieces = 0, []
    for kt in order:
        first = max(0, kt * P - q0)
        pieces.append((kt, first, nq - first, at))
        at += nq - first
    CHUNKS.append((q0, nq, pieces, at))
PTW = max(c[3] for c in CHUNKS)
NC = len(CHUNKS)
STEPS = NG * NC
UNITS = 2 * GH
DIAG = (((0, 512, 3), (896, 512, 1)), ((1024, 256, 2),), ((1536, 256, 2),))

MAXCH = [(qt, 0, (qt + 1) * P, True, qt) for qt in range(4)]
for qt in range(4, NT):
    MAXCH += [(qt, 0, 512, False, NT + qt - 4), (qt, 512, (qt + 1) * P - 512, True, qt)]
NM = len(MAXCH)
S1_UNITS = 20

W_SCALE = 64.0
W_PART, A_PART = (0, 1, 0), (0, 0, 1)
UW = NF * 2 * RH + 2 * D

MAX0 = GH * NM
HEAD_AT = {0: [("turn", 0), ("turn", 1)], 1: [("qk", 0), ("qk", 1), ("qk", 2), ("qk", 3)], 2: [("v", 0), ("v", 1)]}
MAX_FROM = 3


def moves(head):
    out = [("up", 0, 0, 0, 0), ("router",)]
    for i in range(2 * NS):
        k = 2 * NS - MAX_FROM
        rows = [2 * (max(0, j - MAX_FROM) * (MAX0 // 2) // k) * head for j in (i, i + 1)]
        out += [("up", (i + 1) // 2, (i + 1) % 2, *rows), ("down", i // 2, i % 2)]
        if head:
            out += HEAD_AT.get(i, [])
    return out


def s1_quota(u):
    return min(MAX0, MAX0 * u // (3 * S1_UNITS))


HEAD_USES = [("turn", 0), ("turn", 1), ("qk", 0), ("qk", 1), ("qk", 2), ("qk", 3), ("v", 0), ("v", 1)]


def psum_uses(head):
    st, s1 = [], []
    for n in range(STEPS):
        for u in range(UNITS):
            st.append(("att", n, u))
            if n // NC + 1 < NG:
                at = 3 * (n % NC * UNITS + u)
                s1 += [("max", n // NC + 1, i) for i in range(s1_quota(at), s1_quota(at + 3))]
    st += [(kind, h) for kind in ("ot", "op", "ln") for h in range(2)]
    for kind, *at in moves(head):
        if kind == "up":
            st += [("ffn", at[0], 2 * at[1]), ("ffn", at[0], 2 * at[1] + 1)]
            s1 += [("max", 0, i) for i in range(at[2], at[3])]
        elif kind == "down":
            s1 += [("down", at[0], at[1], t) for t in range(4)]
        elif kind != "router":
            st.append((kind, at[0]))
    st += [("ffn", u, k) for u in range(NS, NU) for k in range(4) if (u, k) > (NS, 1)]
    s1 += [("down", u, c, t) for u in range(NS, NU) for c in range(2) for t in range(4)]
    return st, s1


ST_ORDER, S1_ORDER = {h: psum_uses(h)[0] for h in (True, False)}, {h: psum_uses(h)[1] for h in (True, False)}
ST_AT = {h: {use: i for i, use in enumerate(ST_ORDER[h])} for h in ST_ORDER}
S1_AT = {h: {use: i for i, use in enumerate(S1_ORDER[h])} for h in S1_ORDER}
ST_USES, S1_USES = len(ST_ORDER[True]), len(S1_ORDER[True])
ST_HEAD = len(HEAD_USES)
S1_SETUP = 4
S1_HEAD = S1_SETUP + MAX0
MISC = ["out0", "max1", "out1", "out2", "out3", "max2", "out4", "out5", "out6", "max3",
        "out7", "out8", "out9", "out10", "out11", "router", "max0"]
MISC_AT = {name: i for i, name in enumerate(MISC)}
MISC_USES = len(MISC)
MASKS = sum(len(d) for d in DIAG) * GH * NG
DVE_STEPS = 56
DVE_SETUP = 23
POOL_SET = 7 + NE


def adaln_layer(nc, x, w_qk, w_v, w_o, ffn_w, router_w, bias, c_t, w_mod, out):
    assert ST_USES % 2 == 0 and S1_USES % 2 == 0 and ST_HEAD % 2 == 0 and S1_HEAD % 2 == 0 and STEPS % 2 == 0
    gates_dram = nc.dram_tensor("gates", [B, 2 * D], F32).ap()
    ffn_parts = nc.dram_tensor("ffn_parts", [NU, P, 2 * UW], F16).ap()
    x_v = x.rearrange("b (t p) d -> b p t d", p=P)
    out_v = out.rearrange("b (t p) d -> b p t d", p=P)

    with ExitStack() as ctx:
        def sb(name, shape, dt):
            return ctx.enter_context(nc.sbuf_tensor(name, shape, dt))

        def psum(name, shape, dt):
            return ctx.enter_context(nc.psum_tensor(name, shape, dt))

        def sem(name):
            return ctx.enter_context(nc.semaphore(name))

        probs = sb("probs", [P, 2, GH * PTW], F32)
        q_stack = sb("q_stack", [P, NG, GH, T], BF16)
        k_stack = sb("k_stack", [P, NG, GH, T], BF16)
        x_sb = sb("x_sb", [P, NT, D], F32)
        norm = sb("norm", [P, NT, D], F32)
        feat = sb("feat", [P, NF, T], F32)
        v_sb = sb("v_sb", [P, NT, NH * VW + 16], F32)
        o_tok = sb("o_tok", [P, NT, D], F32)
        small = sb("small", [P, 1024], F32)
        wqk_sb = sb("wqk_sb", [P, NG, NF, P], F32)
        wv_sb = sb("wv_sb", [P, NF, D], F32)
        wo_sb = sb("wo_sb", [P, NF, D], F32)
        rw_sb = sb("rw_sb", [P, NF, NE], F32)
        ffn_sb = sb("ffn_sb", [P, 2, 2, UW], F16)
        shift_rows = sb("shift_rows", [SHIFT * GH, T], BF16)
        gates = sb("gates_sb", [P, 2, D], F32)
        mask = sb("mask", [P, 512], BF16)
        junk = sb("junk", [P, 2, 512], BF16)
        ident = sb("ident", [P, P], F32)
        ident_b = sb("ident_b", [P, P], BF16)
        max_part = sb("max_part", [P, GH, NT + 4], F32)
        max_bf = sb("max_bf", [P, NT, SHIFT, GH], BF16)
        l_inv = sb("l_inv", [P, 4 * GH], F32)
        stats = sb("stats", [P, NT, 6], F32)
        mean_var = sb("mean_var", [P, NT, 2], F32)
        rstd = sb("rstd", [P, 3, NT], F32)
        mod_t = sb("mod_t", [P, B, 8], F32)
        mod_col = sb("mod_col", [P, 2, 4], F32)
        bias_sb = sb("bias_sb", [P, NE], F32)
        desc = sb("desc", [P, NE], F32)
        score = sb("score", [P, NT, NE], F32)
        choice = sb("choice", [P, NT, NE], F32)
        hot = sb("hot", [P, 2, NT, NE], F32)
        peak = sb("peak", [P, NT], F32)
        gate = sb("gate", [P, NE, NT], F32)
        eps = sb("eps", [P, 1], F32)

        wmod_sb = probs[:, 0, 0:NF * 6 * D].rearrange("p (f n) -> p f n", f=NF)
        mod_sb = probs[0:B, 0, 4096:4096 + 6 * D]
        guard = probs[0:B, 0, 6144:6144 + 4 * D].rearrange("p (a m n) -> p a m n", a=2, m=2)
        ct_sb = feat[:, 0, 0:NF * B]
        silu_c = feat[:, 1, 0:NF * B].rearrange("p (f b) -> p f b", f=NF)
        parts = [probs[:, 0, g * 1536:(g + 1) * 1536].bitcast(BF16).rearrange("p (a n) -> p a n", a=3) for g in range(NG)]
        rest = [probs[:, 0, 6 * T:7 * T], probs[:, 1, 0:T]]
        x1 = probs[:, 1, T:3 * T].rearrange("p (t d) -> p t d", t=NT)
        feat1 = probs[:, 1, 3 * T:5 * T].rearrange("p (f n) -> p f n", f=NF)
        feat_parts = probs[:, 1, 5 * T:7 * T].bitcast(F16).rearrange("p (a f n) -> p a f n", a=2, f=NF)
        o_raw = small[:, 0:512]
        silu_h = small[:, :].rearrange("p (a n) -> p a n", a=2)
        hidden = o_tok[:, :, :].rearrange("p t d -> p (t d)").bitcast(F16).rearrange("p (c a h n) -> p c a h n", c=2, a=2, h=2)
        stage = [buf[:, :, :].rearrange("p t d -> p (t d)")[:, 0:UW] for buf in (o_tok, norm)]
        w_up = [[ffn_sb[:, s, a, 0:NF * 2 * RH].rearrange("p (f n) -> p f n", f=NF) for a in range(2)] for s in range(2)]
        w_down = [[ffn_sb[:, s, a, NF * 2 * RH:].rearrange("p (h n) -> p h n", h=2) for a in range(2)] for s in range(2)]

        st = [psum(f"st{i}", [P, 1024], F32) for i in range(2)]
        s1 = [psum(f"s1_{i}", [P, 512], F32) for i in range(2)]
        pv = psum("pv", [P, 512], F32)
        misc = psum("misc", [P, 512], F32)
        misc_b = misc[:, :].bitcast(BF16)

        weights_in, pool_set = sem("weights_in"), sem("pool_set")
        x_in, x1_in, gates_in, out_done = sem("x_in"), sem("x1_in"), sem("gates_in"), sem("out_done")
        w_high, w_low = sem("w_high"), sem("w_low")
        w_stored = [sem(f"w_stored{s}") for s in range(2)]
        stage_in = [sem(f"stage_in{s}") for s in range(2)]
        ffn_in = [sem(f"ffn_in{s}") for s in range(2)]
        stacked = [sem(f"stacked{g}") for g in range(NG)]
        shift_in = sem("shift_in")
        st_full, s1_full, pv_full, misc_full = sem("st_full"), sem("s1_full"), sem("pv_full"), sem("misc_full")
        s1_free, scaled = sem("s1_free"), sem("scaled")
        dve_step, waits_apart = sem("dve_step"), sem("waits_apart")
        var_ready, std_ready = sem("var_ready"), sem("std_ready")
        norm1_ready, norm2_ready = sem("norm1_ready"), sem("norm2_ready")
        mod1_ready, mod2_ready = sem("mod1_ready"), sem("mod2_ready")
        feat_ready, feat1_ready = sem("feat_ready"), sem("feat1_ready")
        feat_high, feat_low = sem("feat_high"), sem("feat_low")
        part0_ready, rest_ready, part1_ready, part2_ready = sem("part0"), sem("rest"), sem("part1"), sem("part2")
        v_ready, max_ready, rows_ready = sem("v_ready"), sem("max_ready"), sem("rows_ready")
        exp_done, masked = sem("exp_done"), sem("masked")
        raw_ready, o_ready = sem("raw_ready"), sem("o_ready")
        score_ready, gate_ready = sem("score_ready"), sem("gate_ready")
        silu_ready, hidden_ready, hidden_high, hidden_low = sem("silu"), sem("hidden_ready"), sem("hidden_high"), sem("hidden_low")
        out_ready = sem("out_ready")
        c_ready, guard_ready = sem("c_ready"), sem("guard_ready")

        block = ctx.enter_context(nc.Block())

        def apart(engine):
            engine.sem_inc(waits_apart, 1)

        def st_at(b, head, use):
            return ST_HEAD + b * ST_USES + ST_AT[head][use]

        def ffn_at(b, head, u, k):
            return b * ST_USES + u * 4 + (ST_HEAD + ST_AT[head][("ffn", NS, 0)] - 4 * NS + k)

        def s1_at(b, head, use):
            return S1_HEAD + b * S1_USES + S1_AT[head][use]

        def down_at(b, head, u, k):
            return b * S1_USES + u * NT + (S1_HEAD + S1_AT[head][("down", NS, 0, 0)] - NT * NS + k)

        def hidden_at(b, u, k):
            return b * (NU * 4) + u * 4 + k

        def misc_at(b, name):
            return 1 + b * MISC_USES + MISC_AT[name]

        def head_st(b, use):
            return HEAD_USES.index(use) if isinstance(b, int) and b == 0 else st_at(b - 1, True, use)

        def head_max(b, i):
            return S1_SETUP + i if isinstance(b, int) and b == 0 else s1_at(b - 1, True, ("max", 0, i))

        STACK = 16 * 2 * len(Q_PART)

        @block.sync
        def _(sp):
            loads = ((ct_sb, c_t), (wmod_sb, w_mod), (wqk_sb[:, :, :, :], w_qk), (wv_sb[:, :, :], w_v),
                     (wo_sb[:, :, :], w_o), (rw_sb[:, :, :], router_w), (bias_sb[:, :], bias))

            def load_x1(b):
                sp.dma_start(x1, x_v[bass.ds(b, 1)].rearrange("o p t d -> (o p) t d")).then_inc(x1_in, 16)

            def stack(b, g):
                sp.wait_ge(part2_ready, b * NG + (g + 1))
                for i in range(len(Q_PART)):
                    rows = slice(HD * i, HD * i + HD)
                    sp.dma_start(q_stack[rows, g, :, :], parts[g][0:64, Q_PART[i], :]).then_inc(stacked[g], 16)
                    sp.dma_start(k_stack[rows, g, :, :], parts[g][64:128, K_PART[i], :]).then_inc(stacked[g], 16)

            def shift(b, g):
                sp.wait_ge(rows_ready, b * NG + (g + 1))
                sp.dma_start(q_stack[KS:KS + SHIFT, g, :, :], shift_rows[:, :]).then_inc(shift_in, 16)

            def load_unit(u, s):
                sp.dma_start(ffn_sb[:, s, :, :], ffn_parts[bass.ds(u, 1)].rearrange("o p n -> (o p) n")).then_inc(ffn_in[s], 16)

            def batch(b, head):
                sp.wait_ge(out_ready, b + 1)
                sp.dma_start(x_sb[:, :, :], x_v[bass.ds(b, 1)].rearrange("o p t d -> (o p) t d")).then_inc(x_in, 16)
                sp.dma_start(gates[:, :, :].rearrange("p m n -> p (m n)"),
                             gates_dram[bass.ds(b, 1), :].to_broadcast([P, 2 * D])).then_inc(gates_in, 16)
                for s in range(2):
                    load_unit(s, s)
                for g in range(1, NG):
                    shift(b, g)
                if head:
                    sp.wait_ge(pv_full, (b + 1) * STEPS)
                    load_x1(b + 1)
                for u in range(2, NS + 2):
                    sp.wait_ge(s1_free, s1_at(b, head, ("down", u - 2, 1, 3)) + 1)
                    load_unit(u, u % 2)
                    if u == 2 and head:
                        for g in range(NG):
                            stack(b + 1, g)
                with sp.Fori(NS // 2 + 1, NU // 2) as pair:
                    for s in range(2):
                        sp.wait_ge(s1_free, down_at(b, head, pair * 2, (s - 2) * NT + NT))
                        load_unit(pair * 2 + s, s)
                if head:
                    shift(b + 1, 0)
                sp.wait_ge(out_ready, b + 2)
                sp.dma_start(out_v[bass.ds(b, 1)].rearrange("o p t d -> (o p) t d"), norm[:, :, :]).then_inc(out_done, 16)

            for dst, src in loads:
                sp.dma_start(dst, src).then_inc(weights_in, 16)
            load_x1(0)
            for u in range(2):
                sp.dma_start(stage[u], ffn_w[u]).then_inc(stage_in[u], 16)
            sp.wait_ge(guard_ready, 1)
            sp.dma_start(gates_dram, guard[:, 0, :, :]).then_inc(out_done, 16)
            sp.wait_ge(out_done, 16)
            for g in range(NG):
                stack(0, g)
            for u in range(NU):
                if u == NU // 2:
                    shift(0, 0)
                sp.wait_ge(w_low, u + 1)
                sp.dma_start(ffn_parts[u], ffn_sb[:, u % 2, :, :].rearrange("p a n -> p (a n)")).then_inc(w_stored[u % 2], 16)
                if u + 2 < NU:
                    sp.dma_start(stage[u % 2], ffn_w[u + 2]).then_inc(stage_in[u % 2], 16)
            for s in range(2):
                sp.wait_ge(w_stored[s], 16 * (NU // 2))
            with sp.Fori(0, B - 1) as b:
                batch(b, True)
            batch(B - 1, False)
            sp.wait_ge(out_done, 16 * (B + 1))

        @block.gpsimd
        def _(pool):
            gp = nc.gpsimd
            gp.memset(ident[:, :], 0.0).then_inc(pool_set, 1)
            gp.memset(mask[:, :], 0.0).then_inc(pool_set, 1)
            gp.memset(v_sb[:, :, :], 1.0).then_inc(pool_set, 1)
            gp.memset(eps[:, :], EPS).then_inc(pool_set, 1)
            for e in range(NE):
                gp.memset(desc[:, e:e + 1], float(NE - e)).then_inc(pool_set, 1)
            pool.wait_ge(pool_set, 4 + NE)
            gp.affine_select(ident[:, :], ident[:, :], [[-1, P]], ALU.not_equal, 1.0, 0, 1).then_inc(pool_set, 1)
            gp.affine_select(mask[:, 384:512], mask[:, 384:512], [[-1, P]], ALU.is_ge, NEG, 0, 1).then_inc(pool_set, 1)
            pool.wait_ge(pool_set, 6 + NE)
            gp.tensor_copy(ident_b[:, :], ident[:, :]).then_inc(pool_set, 1)

            def part2(b, g):
                pool.wait_ge(part1_ready, b * NG + (g + 1))
                gp.tensor_tensor(parts[g][:, 2, :], rest[g % 2], parts[g][:, 1, :], ALU.subtract).then_inc(part2_ready, 1)

            def low(b, u, k):
                pool.wait_ge(hidden_high, hidden_at(b, u, k + 1))
                gp.tensor_tensor(hidden[:, k // 2, 1, k % 2, :], silu_h[:, k % 2, :], hidden[:, k // 2, 0, k % 2, :],
                                 ALU.subtract).then_inc(hidden_low, 1)

            def batch(b, head):
                for n in range(STEPS):
                    c = n % NC
                    for j in range(GH):
                        pool.wait_ge(exp_done, b * STEPS * UNITS + (n * UNITS + 2 * j + 2))
                        apart(pool)
                        row = probs[:, n % 2, j * PTW:(j + 1) * PTW]
                        for at, step, k in DIAG[c]:
                            v = row[:, at:at + step * (k - 1) + P].rearrange("p (m n) -> p m n", n=P)[:, 0::step // P, :]
                            gp.affine_select(v, v, [[0, k], [1, P]], ALU.is_ge, 0.0, 0, -1).then_inc(masked, 1)
                for kind, *at in moves(head):
                    if kind == "up":
                        for k in range(2):
                            low(b, at[0], 2 * at[1] + k)
                    elif kind == "qk":
                        part2(b + 1, at[0])
                for k in range(2, 4):
                    low(b, NS, k)
                with pool.Fori(NS + 1, NU) as u:
                    for k in range(4):
                        low(b, u, k)

            for _ in range(2):
                pool.sem_inc(hidden_low, 1)
            for g in range(NG):
                part2(0, g)
            with pool.Fori(0, B - 1) as b:
                batch(b, True)
            batch(B - 1, False)

        @block.scalar
        def _(act):
            sc = nc.scalar
            act.wait_ge(weights_in, 16 * 7)
            sc.activation(silu_c.rearrange("p f b -> p (f b)"), ct_sb, ACT.Silu).then_inc(c_ready, 1)
            act.wait_ge(pool_set, POOL_SET)

            def norm_std(order):
                act.wait_ge(var_ready, order)
                sc.activation(rstd[:, 0, :], mean_var[:, :, 1], ACT.Sqrt, bias=eps[:, 0:1]).then_inc(std_ready, 1)

            def modulate(to, k, f, done):
                return sc.activation(to[0][:, f, :], to[1], ACT.Identity, bias=mod_col[:, k, f:f + 1],
                                     scale=mod_col[:, k, 2 + f:3 + f]).then_inc(done, 1)

            def turn1(b, f):
                at = head_st(b, ("turn", f))
                act.wait_ge(st_full, at + 1)
                modulate((feat1, st[HEAD_USES.index(("turn", f)) % 2][:, :]), 0, f, feat1_ready)

            def part0(b, g):
                act.wait_ge(st_full, head_st(b, ("qk", g)) + 1)
                sc.activation(parts[g][:, 0, :], st[HEAD_USES.index(("qk", g)) % 2][:, :], ACT.Copy).then_inc(part0_ready, 1)

            def part1(b, g):
                act.wait_ge(rest_ready, b * NG + (g + 1))
                sc.activation(parts[g][:, 1, :], rest[g % 2], ACT.Copy).then_inc(part1_ready, 1)

            def shift_copy(b, g, count):
                act.wait_ge(misc_full, count)
                if g >= 1 or not (isinstance(b, int) and b == 0):
                    act.wait_ge(shift_in, b * (NG * 16) + g * 16)
                sc.activation(shift_rows[:, :], misc_b[0:SHIFT * GH, :], ACT.Copy).then_inc(rows_ready, 1)

            def raw_copy(b, n):
                nq = CHUNKS[n % NC][1]
                act.wait_ge(pv_full, b * STEPS + (n + 1))
                if n >= 1:
                    act.wait_ge(misc_full, misc_at(b, f"out{n - 1}") + 1)
                sc.activation(o_raw[:, 0:nq], pv[:, 0:nq], ACT.Copy).then_inc(raw_ready, 1)

            def exps(b, head, n, u):
                c, j, t = n % NC, u // 2, u % 2
                w = (1024, CHUNKS[c][3] - 1024)[t]
                act.wait_ge(st_full, st_at(b, head, ("att", n, u)) + 1)
                at = j * PTW + 1024 * t
                sc.activation(probs[:, n % 2, at:at + w], st[u % 2][:, 0:w], ACT.Exp, scale=SCALE).then_inc(exp_done, 1)

            def hide(b, u, c, full):
                for k in (2 * c, 2 * c + 1):
                    act.wait_ge(st_full, full(k) + 1)
                    act.wait_ge(hidden_low, hidden_at(b, u, k + 1))
                    sc.activation(silu_h[:, k % 2, :], st[k % 2][:, 0:512], ACT.Silu, scale=1.0 / W_SCALE).then_inc(silu_ready, 1)
                for k in (2 * c, 2 * c + 1):
                    act.wait_ge(hidden_ready, hidden_at(b, u, k + 3))
                    sc.activation(hidden[:, c, 0, k % 2, :], silu_h[:, k % 2, :], ACT.Copy).then_inc(hidden_high, 1)

            def batch(b, head):
                for g in range(NG):
                    act.wait_ge(stacked[g], (b + 1) * STACK)
                for n in range(STEPS):
                    if n >= 2:
                        act.wait_ge(pv_full, b * STEPS + (n - 1))
                    for u in range(UNITS):
                        exps(b, head, n, u)
                    if n >= 1:
                        raw_copy(b, n - 1)
                    if n % NC == NC - 1 and n // NC + 1 < NG:
                        shift_copy(b, n // NC + 1, misc_at(b, f"max{n // NC + 1}") + 1)
                raw_copy(b, STEPS - 1)
                for f in range(NF):
                    act.wait_ge(st_full, st_at(b, head, ("ot", f)) + 1)
                    sc.activation(feat[:, f, :], st[ST_AT[head][("ot", f)] % 2][:, :], ACT.Copy).then_inc(feat_ready, 1)
                norm_std(b * 2 + 2)
                act.wait_ge(mod2_ready, b + 1)
                for f in range(NF):
                    act.wait_ge(st_full, st_at(b, head, ("ln", f)) + 1)
                    modulate((feat, st[ST_AT[head][("ln", f)] % 2][:, :]), 1, f, feat_ready)
                    act.wait_ge(feat_ready, b * 2 * NF + (NF + f + 1))
                    sc.activation(feat_parts[:, 0, f, :], feat[:, f, :], ACT.Copy).then_inc(feat_high, 1)
                if head:
                    norm_std(b * 2 + 3)
                    act.wait_ge(mod1_ready, b + 2)
                for kind, *at in moves(head):
                    if kind == "up":
                        hide(b, at[0], at[1], lambda k: st_at(b, head, ("ffn", at[0], k)))
                    elif kind == "router":
                        act.wait_ge(misc_full, misc_at(b, "router") + 1)
                        sc.activation(score[:, :, :].rearrange("p t e -> p (t e)"), misc[:, 0:NT * NE], ACT.Sigmoid).then_inc(score_ready, 1)
                    elif kind == "turn":
                        turn1(b + 1, at[0])
                    elif kind == "qk":
                        part0(b + 1, at[0])
                        if at[0] >= 1:
                            part1(b + 1, at[0] - 1)
                        if at[0] == NG - 1:
                            part1(b + 1, at[0])
                hide(b, NS, 1, lambda k: ffn_at(b, head, NS, k))
                with act.Fori(NS + 1, NU) as u:
                    for c in range(2):
                        hide(b, u, c, lambda k: ffn_at(b, head, u, k))
                if head:
                    shift_copy(b + 1, 0, misc_at(b, "max0") + 1)

            norm_std(1)
            act.wait_ge(mod1_ready, 1)
            act.wait_ge(out_done, 16)
            for f in range(NF):
                turn1(0, f)
            for g in range(NG + 1):
                if g < NG:
                    part0(0, g)
                if g >= 1:
                    part1(0, g - 1)
            for u in range(NU):
                if u == NU // 2:
                    shift_copy(0, 0, 1)
                act.wait_ge(stage_in[u % 2], 16 * (u // 2 + 1))
                if u >= 2:
                    act.wait_ge(w_stored[u % 2], 16 * (u // 2))
                sc.activation(ffn_sb[:, u % 2, 0, :], stage[u % 2], ACT.Copy, scale=W_SCALE).then_inc(w_high, 1)
            with act.Fori(0, B - 1) as b:
                batch(b, True)
            batch(B - 1, False)

        @block.vector
        def _(dve):
            vec = nc.vector
            count = [0]

            def chain(ins, base):
                count[0] += 1
                ins.then_inc(dve_step, 1)
                dve.wait_ge(dve_step, base + count[0])

            def spread(b, k, base, x_of):
                for t in range(NT):
                    vec.bn_stats(stats[:, t, :], x_of[:, t, :]).then_inc(dve_step, 1)
                    count[0] += 1
                dve.wait_ge(dve_step, base + count[0])
                apart(dve)
                for t in range(NT):
                    ins = vec.bn_aggr(mean_var[:, t, :], stats[:, t, :])
                ins.then_inc(var_ready, 1)

            def normed(order, base, to, x_of, done):
                dve.wait_ge(std_ready, order)
                chain(vec.reciprocal(rstd[:, 1, :], rstd[:, 0, :]), base)
                chain(vec.scalar_tensor_tensor(rstd[:, 2, :], mean_var[:, :, 0], -1.0, rstd[:, 1, :], ALU.mult, ALU.mult), base)
                for t in range(NT):
                    vec.tensor_scalar(to[:, t, :], x_of[:, t, :], rstd[:, 1, t:t + 1], rstd[:, 2, t:t + 1],
                                      ALU.mult, ALU.add).then_inc(done, 1)

            def mod_copy(b, k, done):
                vec.tensor_copy(mod_col[:, k, :], mod_t[:, bass.ds(b, 1), 4 * k:4 * k + 4].rearrange("p o k -> p (o k)")).then_inc(done, 1)

            def split(b, g):
                dve.wait_ge(part0_ready, b * NG + (g + 1))
                if g >= 2:
                    dve.wait_ge(part2_ready, b * NG + (g - 1))
                vec.tensor_tensor(rest[g % 2], st[HEAD_USES.index(("qk", g)) % 2][:, :], parts[g][:, 0, :], ALU.subtract).then_inc(rest_ready, 1)

            def take_v(b, h):
                dve.wait_ge(st_full, head_st(b, ("v", h)) + 1)
                for t in range(4):
                    to = v_sb[:, 4 * h + t, 0:NH * VW].rearrange("p (h d) -> p h d", d=VW)[:, :, 0:HD]
                    vec.tensor_copy(to, st[h % 2][:, t * D:(t + 1) * D].rearrange("p (h d) -> p h d", d=HD)).then_inc(v_ready, 1)

            def maxima(g, i0, i1, at):
                for i in range(i0, i1):
                    j, (qt, k0, nk, masked_, col) = i // NM, MAXCH[i % NM]
                    dve.wait_ge(s1_full, at(i) + 1)
                    dve.wait_ge(s1_free, at(i) - 1)
                    tile, to = s1[i % 2], max_part[:, j, col:col + 1]
                    if masked_:
                        apart(dve)
                        vec.tensor_tensor_reduce(junk[:, i % 2, 0:nk], tile[:, 0:nk], mask[:, 512 - nk:512], 1.0, NEG,
                                                 ALU.add, ALU.max, to).then_inc(s1_free, 1)
                    else:
                        vec.tensor_reduce(to, tile[:, 0:nk], AX.X, ALU.max).then_inc(s1_free, 1)

            def shifts(last, base):
                dve.wait_ge(s1_free, last + 1)
                hi = max_part[:, :, 4:NT]
                chain(vec.tensor_tensor(hi, hi, max_part[:, :, NT:NT + 4], ALU.max), base)
                m = max_part[:, :, 0:NT]
                parts_of = [max_bf[:, :, a, :].rearrange("p t j -> p j t") for a in range(SHIFT)]
                chain(vec.tensor_scalar(parts_of[0], m, -1.0, None, ALU.mult), base)
                vec.scalar_tensor_tensor(parts_of[1], m, -1.0, parts_of[0], ALU.mult, ALU.subtract).then_inc(max_ready, 1)

            def normalise(b, n, base):
                c = n % NC
                q0, nq = CHUNKS[c][:2]
                k = nq // P * GH
                dve.wait_ge(misc_full, misc_at(b, f"out{n}") + 1)
                o = misc[:, 0:k * 32].rearrange("p (k n) -> p k n", k=k)
                chain(vec.reciprocal(l_inv[:, 0:k], o[:, :, HD]), base)
                h0 = n // NC * GH * HD
                to = o_tok[:, q0 // P:(q0 + nq) // P, h0:h0 + GH * HD].rearrange("p t (j d) -> p t j d", j=GH)
                vec.tensor_tensor(to, o[:, :, 0:HD].rearrange("p (t j) d -> p t j d", j=GH),
                                  l_inv[:, 0:k].rearrange("p (t j) -> p t j", j=GH).unsqueeze(3).to_broadcast([P, nq // P, GH, HD]),
                                  ALU.mult).then_inc(o_ready, 1)

            def hide(b, u, k):
                dve.wait_ge(silu_ready, hidden_at(b, u, k + 1))
                vec.scalar_tensor_tensor(silu_h[:, k % 2, :], st[k % 2][:, 512:1024], 1.0 / W_SCALE, silu_h[:, k % 2, :],
                                         ALU.mult, ALU.mult).then_inc(hidden_ready, 1)

            def add_up(u, c, t0, t1, at):
                for t in range(t0, t1):
                    dve.wait_ge(s1_full, at(t) + 1)
                    y, total = s1[t % 2][:, 0:D], norm[:, c * 4 + t, :]
                    if isinstance(u, int) and u == 0:
                        vec.tensor_copy(total, y).then_inc(s1_free, 1)
                    elif isinstance(u, int) and u < NS:
                        vec.tensor_tensor(total, y, total, ALU.add).then_inc(s1_free, 1)
                    else:
                        vec.scalar_tensor_tensor(total, y, gate[:, bass.ds(u - NS, 1), c * 4 + t], total, ALU.mult, ALU.add).then_inc(s1_free, 1)

            def route(b, base):
                dve.wait_ge(score_ready, b + 1)

                def wide(a):
                    return a.unsqueeze(2).to_broadcast([P, NT, NE])

                chain(vec.tensor_tensor(choice[:, :, :], score[:, :, :], bias_sb[:, :].unsqueeze(1).to_broadcast([P, NT, NE]), ALU.add), base)
                for r in range(2):
                    chain(vec.tensor_reduce(peak[:, :], choice[:, :, :], AX.X, ALU.max), base)
                    chain(vec.tensor_tensor(hot[:, r, :, :], choice[:, :, :], wide(peak[:, :]), ALU.is_equal), base)
                    chain(vec.tensor_tensor(hot[:, r, :, :], hot[:, r, :, :], desc[:, :].unsqueeze(1).to_broadcast([P, NT, NE]), ALU.mult), base)
                    chain(vec.tensor_reduce(peak[:, :], hot[:, r, :, :], AX.X, ALU.max), base)
                    chain(vec.tensor_tensor(hot[:, r, :, :], hot[:, r, :, :], wide(peak[:, :]), ALU.is_equal), base)
                    if r == 0:
                        chain(vec.scalar_tensor_tensor(choice[:, :, :], hot[:, 0, :, :], NEG, choice[:, :, :], ALU.mult, ALU.add), base)
                chain(vec.tensor_tensor(hot[:, 0, :, :], hot[:, 0, :, :], hot[:, 1, :, :], ALU.add), base)
                vec.tensor_tensor(gate[:, :, :].rearrange("p e t -> p t e"), hot[:, 0, :, :], score[:, :, :], ALU.mult).then_inc(gate_ready, 1)

            def batch(b, head):
                count[0] = 0
                base = b * DVE_STEPS + DVE_SETUP
                for n in range(STEPS):
                    g, c = n // NC, n % NC
                    for u in range(UNITS):
                        if g + 1 < NG:
                            x = 3 * (c * UNITS + u)
                            maxima(g + 1, s1_quota(x), s1_quota(x + 3), lambda i: s1_at(b, head, ("max", g + 1, i)))
                        if u == 2 and n >= 2:
                            normalise(b, n - 2, base)
                    if c == NC - 1 and g + 1 < NG:
                        shifts(s1_at(b, head, ("max", g + 1, MAX0 - 1)), base)
                normalise(b, STEPS - 2, base)
                mod_copy(b, 1, mod2_ready)
                normalise(b, STEPS - 1, base)
                dve.wait_ge(x_in, (b + 1) * 16)
                dve.wait_ge(gates_in, (b + 1) * 16)
                for h in range(2):
                    dve.wait_ge(st_full, st_at(b, head, ("op", h)) + 1)
                    y = o_tok[:, 4 * h:4 * h + 4, :]
                    vec.tensor_tensor(y, st[ST_AT[head][("op", h)] % 2][:, :].rearrange("p (t d) -> p t d", d=D),
                                      gates[:, 0, :].unsqueeze(1).to_broadcast([P, 4, D]), ALU.mult).then_inc(scaled, 1)
                    dve.wait_ge(scaled, b * 2 + (h + 1))
                    chain(vec.tensor_tensor(x_sb[:, 4 * h:4 * h + 4, :], x_sb[:, 4 * h:4 * h + 4, :], y, ALU.add), base)
                spread(b, 1, base, x_sb)
                dve.wait_ge(out_done, (b + 1) * 16)
                normed(b * 2 + 2, base, norm, x_sb, norm2_ready)
                for f in range(NF):
                    dve.wait_ge(feat_high, b * NF + (f + 1))
                    vec.tensor_tensor(feat_parts[:, 1, f, :], feat[:, f, :], feat_parts[:, 0, f, :], ALU.subtract).then_inc(feat_low, 1)
                if head:
                    mod_copy(b + 1, 0, mod1_ready)
                    dve.wait_ge(x1_in, (b + 2) * 16)
                    spread(b + 1, 0, base, x1)
                for kind, *at in moves(head):
                    if kind == "up":
                        u, c, i0, i1 = at
                        half = i0 + (i1 - i0) * 2 // 3
                        maxima(0, i0, half, lambda i: head_max(b + 1, i))
                        hide(b, u, 2 * c)
                        maxima(0, half, i1, lambda i: head_max(b + 1, i))
                        if u + c == 0:
                            hide(b, 0, 1)
                    elif kind == "down":
                        add_up(*at, 0, 2, lambda t: s1_at(b, head, ("down", *at, t)))
                        hide(b, u, 2 * c + 1)
                        add_up(*at, 2, 4, lambda t: s1_at(b, head, ("down", *at, t)))
                        if at == [0, 0]:
                            route(b, base)
                    elif kind == "router":
                        if head:
                            normed(b * 2 + 3, base, x1, x1, norm1_ready)
                    elif kind == "qk":
                        split(b + 1, at[0])
                    elif kind == "v":
                        take_v(b + 1, at[0])
                if head:
                    shifts(head_max(b + 1, MAX0 - 1), base)
                dve.wait_ge(gate_ready, b + 1)
                apart(dve)
                with dve.Fori(NS, NU - 1) as u:
                    for c in range(2):
                        hide(b, u + c, 2 - 2 * c)
                        add_up(u, c, 0, 2, lambda t: down_at(b, head, u, 4 * c + t))
                        hide(b, u + c, 3 - 2 * c)
                        add_up(u, c, 2, 4, lambda t: down_at(b, head, u, 4 * c + t))
                hide(b, NU - 1, 2)
                add_up(NU - 1, 0, 0, 2, lambda t: s1_at(b, head, ("down", NU - 1, 0, t)))
                hide(b, NU - 1, 3)
                add_up(NU - 1, 0, 2, 4, lambda t: s1_at(b, head, ("down", NU - 1, 0, t)))
                add_up(NU - 1, 1, 0, 4, lambda t: s1_at(b, head, ("down", NU - 1, 1, t)))
                dve.wait_ge(s1_free, s1_at(b, head, ("down", NU - 1, 1, 3)) + 1)
                chain(vec.scalar_tensor_tensor(norm[:, :, :], norm[:, :, :], 1.0 / W_SCALE,
                                               gates[:, 1, :].unsqueeze(1).to_broadcast([P, NT, D]), ALU.mult, ALU.mult), base)
                vec.tensor_tensor(norm[:, :, :], norm[:, :, :], x_sb[:, :, :], ALU.add).then_inc(out_ready, 1)
                dve.wait_ge(out_ready, b + 2)
                assert not head or count[0] == DVE_STEPS, count[0]

            for s in (out_ready, raw_ready, hidden_ready, hidden_ready):
                dve.sem_inc(s, 1)
            vec.memset(k_stack[KS:KS + SHIFT, :, :, :], 1.0).then_inc(dve_step, 1)
            count[0] += 1
            for k in range(3):
                dve.wait_ge(s1_full, k + 1)
                vec.tensor_copy(mod_sb[:, k * 512:(k + 1) * 512], s1[k % 2][0:B, :]).then_inc(s1_free, 1)
            dve.wait_ge(s1_free, 3)
            for m, idx in ((0, 2), (1, 5)):
                g = mod_sb[:, idx * D:(idx + 1) * D]
                chain(vec.tensor_scalar(guard[:, 0, m, :], g, 0.0, 2.0, ALU.is_ge, ALU.mult), 0)
                vec.scalar_tensor_tensor(guard[:, 1, m, :], g, -1.0, g, ALU.mult, ALU.max).then_inc(dve_step, 1)
                count[0] += 1
                chain(vec.tensor_scalar(guard[:, 0, m, :], guard[:, 0, m, :], -1.0, None, ALU.add), 0)
                ins = vec.scalar_tensor_tensor(guard[:, 0, m, :], guard[:, 1, m, :], 0.25, guard[:, 0, m, :], ALU.max, ALU.mult)
                if m == 0:
                    chain(ins, 0)
                else:
                    ins.then_inc(guard_ready, 1)
            dve.wait_ge(s1_full, 4)
            mt = mod_t[:, :, :].rearrange("p b k -> p k b")
            ps = s1[1][:, 0:8 * B].rearrange("p (k b) -> p k b", k=8)
            for i, add in ((0, 0.0), (2, 1.0), (4, 0.0)):
                vec.tensor_scalar(mt[:, i:i + 2, :], ps[:, i:i + 2, :], add, None, ALU.add).then_inc(dve_step, 1)
                count[0] += 1
            vec.tensor_scalar(mt[:, 6:8, :], ps[:, 6:8, :], 1.0, None, ALU.add).then_inc(s1_free, 1)
            dve.wait_ge(s1_free, 4)
            mod_copy(0, 0, mod1_ready)
            dve.wait_ge(pool_set, POOL_SET)
            dve.wait_ge(x1_in, 16)
            spread(0, 0, 0, x1)
            normed(1, 0, x1, x1, norm1_ready)
            for g in range(NG):
                split(0, g)
            for h in range(2):
                take_v(0, h)
            maxima(0, 0, MAX0, lambda i: head_max(0, i))
            shifts(head_max(0, MAX0 - 1), 0)
            for u in range(NU):
                dve.wait_ge(w_high, u + 1)
                vec.scalar_tensor_tensor(ffn_sb[:, u % 2, 1, :], stage[u % 2], W_SCALE, ffn_sb[:, u % 2, 0, :],
                                         ALU.mult, ALU.subtract).then_inc(w_low, 1)
            assert count[0] == DVE_SETUP, count[0]
            with dve.Fori(0, B - 1) as b:
                batch(b, True)
            batch(B - 1, False)

        @block.tensor
        def _(pe):
            mm = nc.tensor.matmul
            pe.wait_ge(c_ready, 1)
            pe.wait_ge(pool_set, POOL_SET)
            for k in range(3):
                if k >= 2:
                    pe.wait_ge(s1_free, k - 1)
                for f in range(NF):
                    last = mm(s1[k % 2][0:B, :], silu_c[:, f, :], wmod_sb[:, f, k * 512:(k + 1) * 512], start=(f == 0), stop=(f == NF - 1))
                last.then_inc(s1_full, 1)
            pe.wait_ge(s1_free, 3)
            for i, idx in enumerate((0, 1, 3, 4)):
                for f in range(NF):
                    k = 2 * i + f
                    last = nc.tensor.transpose(s1[1][:, k * B:(k + 1) * B], mod_sb[:, idx * D + f * P:idx * D + (f + 1) * P], ident[0:B, 0:B])
            last.then_inc(s1_full, 1)

            def st_read(b, use):
                kind, i = use[0], use[1]
                if kind == "turn":
                    pe.wait_ge(feat1_ready, b * NF + (i + 1))
                elif kind == "qk":
                    pe.wait_ge(rest_ready, b * NG + (i + 1))
                elif kind == "v":
                    pe.wait_ge(v_ready, b * NT + (4 * i + 4))
                elif kind == "att":
                    pe.wait_ge(exp_done, b * STEPS * UNITS + (i * UNITS + use[2] + 1))
                elif kind == "ot":
                    pe.wait_ge(feat_ready, b * 2 * NF + (i + 1))
                elif kind == "op":
                    pe.wait_ge(scaled, b * 2 + (i + 1))
                elif kind == "ln":
                    pe.wait_ge(feat_ready, b * 2 * NF + (NF + i + 1))
                else:
                    pe.wait_ge(hidden_ready, hidden_at(b, i, use[2] + 3))

            def st_use(b, head, use):
                i = ST_AT[head][use]
                if i >= 2:
                    old = ST_ORDER[head][i - 2]
                    st_read(b + 1 if old[0] in ("turn", "qk", "v") else b, old)
                else:
                    pe.wait_ge(hidden_ready, hidden_at(b, 0, i + 1))
                return st[i % 2]

            def head_use(b, use):
                if isinstance(b, int) and b == 0:
                    i = HEAD_USES.index(use)
                    if i >= 2:
                        st_read(0, HEAD_USES[i - 2])
                    return st[i % 2]
                return st_use(b - 1, True, use)

            def misc_use(b, name):
                before = MISC[MISC_AT[name] - 1]
                if name == MISC[0]:
                    pe.wait_ge(rows_ready, b * NG + 1)
                elif before == "router":
                    pe.wait_ge(score_ready, b + 1)
                elif before.startswith("max"):
                    pe.wait_ge(rows_ready, b * NG + (int(before[3:]) + 1))
                else:
                    pe.wait_ge(o_ready, b * STEPS + (int(before[3:]) + 1))

            def turn(to, src, f, ready, need):
                for t in range(NT):
                    pe.wait_ge(ready, need(t))
                    last = nc.tensor.transpose(to[:, t * P:(t + 1) * P], src[:, t, f * P:(f + 1) * P], ident[:, :])
                last.then_inc(st_full, 1)

            def turn1(b, f):
                turn(head_use(b, ("turn", f)), x1, f, norm1_ready, lambda t: b * NT + (t + 1))

            def qk(b, g):
                to = head_use(b, ("qk", g))
                pe.wait_ge(feat1_ready, b * NF + NF)
                for c in range(2):
                    for f in range(NF):
                        last = mm(to[:, c * 512:(c + 1) * 512], wqk_sb[:, g, f, :], feat1[:, f, c * 512:(c + 1) * 512],
                                  start=(f == 0), stop=(f == NF - 1))
                last.then_inc(st_full, 1)

            def make_v(b, h):
                to = head_use(b, ("v", h))
                for t in range(4):
                    for f in range(NF):
                        last = mm(to[:, t * D:(t + 1) * D], feat1[:, f, (4 * h + t) * P:(4 * h + t + 1) * P], wv_sb[:, f, :],
                                  start=(f == 0), stop=(f == NF - 1))
                last.then_inc(st_full, 1)

            def max_rows(g, i0, i1, at):
                for i in range(i0, i1):
                    j, (qt, k0, nk, _, _) = i // NM, MAXCH[i % NM]
                    pe.wait_ge(s1_free, at(i) - 1)
                    mm(s1[i % 2][:, 0:nk], q_stack[0:KS, g, j, qt * P:(qt + 1) * P], k_stack[0:KS, g, j, k0:k0 + nk],
                       start=True, stop=True).then_inc(s1_full, 1)

            def max_turn(b, g):
                pe.wait_ge(max_ready, b * NG + (g + 1))
                if g >= 1:
                    misc_use(b, f"max{g}")
                elif not isinstance(b, int) or b > 0:
                    misc_use(b - 1, "max0")
                for qt in range(NT):
                    last = nc.tensor.transpose(misc_b[0:SHIFT * GH, qt * P:(qt + 1) * P],
                                               max_bf[:, qt, :, :].rearrange("p a j -> p (a j)"), ident_b[:, :])
                last.then_inc(misc_full, 1)

            def scores(b, head, n, u):
                g, c, j, t = n // NC, n % NC, u // 2, u % 2
                q0, nq, pieces, _ = CHUNKS[c]
                to = st_use(b, head, ("att", n, u))
                for kt, first, w, at in pieces:
                    if at // 1024 == t:
                        last = mm(to[:, at % 1024:at % 1024 + w], k_stack[0:KS + SHIFT, g, j, kt * P:(kt + 1) * P],
                                  q_stack[0:KS + SHIFT, g, j, q0 + first:q0 + nq], start=True, stop=True)
                last.then_inc(st_full, 1)

            def values(b, n, k0, k1):
                g, c = n // NC, n % NC
                _, nq, pieces, _ = CHUNKS[c]
                tiles = sorted(pieces)
                if k1 == k0:
                    return
                if k0 == 0:
                    pe.wait_ge(exp_done, b * STEPS * UNITS + (n + 1) * UNITS)
                    pe.wait_ge(masked, b * MASKS + sum(len(DIAG[i % NC]) * GH for i in range(n + 1)))
                    pe.wait_ge(raw_ready, b * STEPS + (n + 1))
                for kt, first, w, at in tiles[k0:k1]:
                    for j in range(GH):
                        h = (g * GH + j) * VW
                        last = mm(pv[32 * j:32 * j + 32, first:nq], v_sb[:, kt, h:h + 32],
                                  probs[:, n % 2, j * PTW + at:j * PTW + at + w], start=(kt == 0), stop=(kt == len(tiles) - 1))
                if k1 >= len(tiles):
                    last.then_inc(pv_full, 1)

            def turn_out(b, n):
                nq = CHUNKS[n % NC][1]
                pe.wait_ge(raw_ready, b * STEPS + (n + 2))
                misc_use(b, f"out{n}")
                for t in range(nq // P):
                    last = nc.tensor.transpose(misc[:, t * P:(t + 1) * P], o_raw[:, t * P:(t + 1) * P], ident[:, :])
                last.then_inc(misc_full, 1)

            def up_half(to, s, c, h, between=None):
                for m in range(2):
                    for i in range(len(W_PART)):
                        for f in range(NF):
                            last = mm(to[:, 512 * m:512 * m + 512], w_up[s][W_PART[i]][:, f, m * RH + h * P:m * RH + (h + 1) * P],
                                      feat_parts[:, A_PART[i], f, c * 512:(c + 1) * 512],
                                      start=(i == 0 and f == 0), stop=(i == len(W_PART) - 1 and f == NF - 1))
                        if m == 1 and i == len(W_PART) - 1:
                            last.then_inc(st_full, 1)
                        if between:
                            between((h * 2 + m) * len(W_PART) + i)

            def up(b, u, c, s):
                for h in range(2):
                    pe.wait_ge(hidden_ready, hidden_at(b, u, 2 * c + h + 1))
                    up_half(st[h], s, c, h)

            def down(b, u, c, s, at):
                pe.wait_ge(hidden_low, hidden_at(b, u, 2 * c + 4))
                for t in range(4):
                    pe.wait_ge(s1_free, at(t) - 1)
                    for i in range(len(W_PART)):
                        for h in range(2):
                            last = mm(s1[t % 2][:, 0:D], hidden[:, c, A_PART[i], h, t * P:(t + 1) * P], w_down[s][W_PART[i]][:, h, :],
                                      start=(i == 0 and h == 0), stop=(i == len(W_PART) - 1 and h == 1))
                    last.then_inc(s1_full, 1)

            def batch(b, head):
                pe.wait_ge(v_ready, (b + 1) * NT)
                for n in range(STEPS):
                    g, c = n // NC, n % NC
                    if c == 0:
                        pe.wait_ge(shift_in, (b * NG + (g + 1)) * 16)
                        if g + 1 < NG:
                            pe.wait_ge(stacked[g + 1], (b + 1) * STACK)
                    for u in range(UNITS):
                        scores(b, head, n, u)
                        if u == 1 and n >= 2:
                            turn_out(b, n - 2)
                        for i in range(3):
                            if g + 1 < NG:
                                x = 3 * (c * UNITS + u) + i
                                max_rows(g + 1, s1_quota(x), s1_quota(x + 1), lambda i: s1_at(b, head, ("max", g + 1, i)))
                            if u >= 2 and n >= 1:
                                k, x = len(CHUNKS[(n - 1) % NC][2]), 3 * (u - 2) + i
                                values(b, n - 1, k * x // 18, k * (x + 1) // 18)
                    if c == NC - 1 and g + 1 < NG:
                        max_turn(b, g + 1)
                values(b, STEPS - 1, 0, NT)
                turn_out(b, STEPS - 2)
                turn_out(b, STEPS - 1)
                for f in range(NF):
                    turn(st_use(b, head, ("ot", f)), o_tok, f, o_ready, lambda t: (b + 1) * STEPS)
                pe.wait_ge(feat_ready, b * 2 * NF + NF)
                for h in range(2):
                    to = st_use(b, head, ("op", h))
                    for t in range(4):
                        for f in range(NF):
                            last = mm(to[:, t * D:(t + 1) * D], feat[:, f, (4 * h + t) * P:(4 * h + t + 1) * P], wo_sb[:, f, :],
                                      start=(f == 0), stop=(f == NF - 1))
                    last.then_inc(st_full, 1)
                for f in range(NF):
                    turn(st_use(b, head, ("ln", f)), norm, f, norm2_ready, lambda t: b * NT + (t + 1))
                pe.wait_ge(feat_low, (b + 1) * NF)
                for kind, *at in moves(head):
                    if kind == "up":
                        u, c, i0, i1 = at
                        if i1 > i0 and i0 == 0:
                            pe.wait_ge(stacked[0], (b + 2) * STACK)

                        def between(x):
                            max_rows(0, i0 + (i1 - i0) * x // 12, i0 + (i1 - i0) * (x + 1) // 12, lambda i: head_max(b + 1, i))

                        if c == 0:
                            pe.wait_ge(ffn_in[u % 2], b * (NU // 2 * 16) + (u // 2 + 1) * 16)
                        for h in range(2):
                            up_half(st_use(b, head, ("ffn", u, 2 * c + h)), u % 2, c, h, between)
                    elif kind == "down":
                        down(b, *at, at[0] % 2, lambda t: s1_at(b, head, ("down", *at, t)))
                    elif kind == "router":
                        misc_use(b, "router")
                        for t in range(NT):
                            for f in range(NF):
                                last = mm(misc[:, t * NE:(t + 1) * NE], feat[:, f, t * P:(t + 1) * P], rw_sb[:, f, :], start=(f == 0), stop=(f == NF - 1))
                        last.then_inc(misc_full, 1)
                    elif kind == "turn":
                        turn1(b + 1, at[0])
                    elif kind == "qk":
                        qk(b + 1, at[0])
                    elif kind == "v":
                        make_v(b + 1, at[0])

                def pair_of_units(u, second_in, third_in):
                    up(b, u, 1, 0)
                    down(b, u, 0, 0, lambda t: down_at(b, head, u, t))
                    pe.wait_ge(ffn_in[1], second_in)
                    up(b, u + 1, 0, 1)
                    down(b, u, 1, 0, lambda t: down_at(b, head, u, 4 + t))
                    up(b, u + 1, 1, 1)
                    down(b, u + 1, 0, 1, lambda t: down_at(b, head, u + 1, t))
                    if third_in is not None:
                        pe.wait_ge(ffn_in[0], third_in)
                        up(b, u + 2, 0, 0)
                    elif head:
                        max_turn(b + 1, 0)
                    down(b, u + 1, 1, 1, lambda t: down_at(b, head, u + 1, 4 + t))

                loaded = b * (NU // 2 * 16)
                with pe.Fori(NS // 2, NU // 2 - 1) as pair:
                    pair_of_units(pair * 2, loaded + pair * 16 + 16, loaded + pair * 16 + 32)
                pair_of_units(NU - 2, loaded + NU // 2 * 16, None)

            for f in range(NF):
                turn1(0, f)
            for g in range(NG):
                qk(0, g)
            for h in range(2):
                make_v(0, h)
            pe.wait_ge(stacked[0], STACK)
            max_rows(0, 0, MAX0, lambda i: head_max(0, i))
            max_turn(0, 0)
            with pe.Fori(0, B - 1) as b:
                batch(b, True)
            batch(B - 1, False)


def kernel(**inputs):
    import numpy as np
    import concourse.bacc as bacc
    from concourse.bass_utils import run_bass_kernel_spmd

    a = {n[3:]: np.asarray(v) for n, v in inputs.items()}
    tight = np.ascontiguousarray
    qkv = a["attn_w_qkv"].reshape(NF, P, NG, GH, 3, HD)
    w_qk = tight(qkv[:, :, :, :, 0:2].transpose(1, 2, 0, 4, 5, 3)).reshape(P, NG, NF, P)
    w_v = tight(qkv[:, :, :, :, 2].transpose(1, 0, 2, 3, 4)).reshape(P, NF, D)
    w_o = tight(a["attn_w_o"].reshape(NF, P, D).transpose(1, 0, 2))

    def unit(w1, w2, w3):
        w_up = np.concatenate([w1, w2], 0).reshape(2 * RH, NF, P).transpose(2, 1, 0).reshape(P, -1)
        w_down = w3.reshape(D, 2, P).transpose(2, 1, 0).reshape(P, -1)
        return np.concatenate([w_up, w_down], 1)

    units = [unit(a["ffn_shared_w1"][h:h + RH], a["ffn_shared_w2"][h:h + RH], a["ffn_shared_w3"][:, h:h + RH]) for h in range(0, SH, RH)]
    units += [unit(a["ffn_w12"][e, :RH], a["ffn_w12"][e, RH:], a["ffn_w3"][e]) for e in range(NE)]
    arrays = {
        "x": tight(a["attn_x"]),
        "w_qk": w_qk, "w_v": w_v, "w_o": w_o,
        "ffn_w": tight(np.stack(units)),
        "router_w": tight(a["ffn_router_w"].reshape(NE, NF, P).transpose(2, 1, 0)),
        "bias": tight(np.broadcast_to(a["ffn_expert_bias"], (P, NE))),
        "c_t": tight(a["c"].reshape(B, NF, P).transpose(2, 1, 0)).reshape(P, NF * B),
        "w_mod": tight(a["wmod"].reshape(NF, P, 6 * D).transpose(1, 0, 2)),
    }
    nc = bacc.Bacc("TRN2", target_bir_lowering=False, num_devices=1)
    args = {n: nc.dram_tensor(n, v.shape, mybir.dt.from_np(v.dtype), kind="ExternalInput").ap() for n, v in arrays.items()}
    args["out"] = nc.dram_tensor("out", (B, T, D), F32, kind="ExternalOutput").ap()
    adaln_layer(nc, **args)
    r = run_bass_kernel_spmd(nc, [arrays], core_ids=[0])
    return r.results[0]["out"]
```

```python
from contextlib import ExitStack

import concourse.bass as bass
from concourse import mybir

ALU = mybir.AluOpType
ACT = mybir.ActivationFunctionType
AX = mybir.AxisListType
F32 = mybir.dt.float32
U32 = mybir.dt.uint32
I32 = mybir.dt.int32
BF16 = mybir.dt.bfloat16
F16 = mybir.dt.float16

P = 128
B, T, D = 8, 1024, 256
NH, HD = 16, 16
NT, NF = T // P, D // P
GH = 4
NG = NH // GH
VW = HD + 1
NE, RH, SH = 8, 256, 1024
NU = SH // RH + NE
NS = SH // RH
EPS = 1e-5
SCALE = 1.0 / 16.0
NEG = -1e30

Q_PART = (0, 0, 1, 0, 1, 2)
K_PART = (0, 1, 0, 2, 1, 0)
KS = HD * len(Q_PART)
SHIFT = 2

CHUNKS = []
for q0, nq, order in ((0, 512, (0, 1, 3, 2)), (512, 256, (0, 1, 2, 3, 4, 5)), (768, 256, (0, 1, 2, 3, 4, 5, 6, 7))):
    at, pieces = 0, []
    for kt in order:
        first = max(0, kt * P - q0)
        pieces.append((kt, first, nq - first, at))
        at += nq - first
    CHUNKS.append((q0, nq, pieces, at))
PTW = max(c[3] for c in CHUNKS)
NC = len(CHUNKS)
STEPS = NG * NC
UNITS = 2 * GH
DIAG = (((0, 512, 3), (896, 512, 1)), ((1024, 256, 2),), ((1536, 256, 2),))

MAXCH = [(qt, 0, (qt + 1) * P, True, qt) for qt in range(4)]
for qt in range(4, NT):
    MAXCH += [(qt, 0, 512, False, NT + qt - 4), (qt, 512, (qt + 1) * P - 512, True, qt)]
NM = len(MAXCH)
HEAD_MAX = 1
STEP_MAX = {1: (0, 3), 2: (3, 6), 3: (6, 9)}

TOPK = 2
ROWS = 512
LIST = B * T + ROWS
TILES = B * T * TOPK // ROWS + NE
WSLOTS = 4

W_SCALE = 64.0
W_PART, A_PART = (0, 1, 0), (0, 0, 1)
UW = NF * 2 * RH + 2 * D

MAX0 = GH * NM
HEAD_AT = {0: [("turn", 0), ("turn", 1)], 1: [("qk", 0), ("qk", 1), ("qk", 2), ("qk", 3)], 2: [("v", 0), ("v", 1)],
           6: [("shift", 0)], 7: [("max_turn", 0)]}
MAX_AT = {0: 3}
MAX_HALVES = 4


def moves(head):
    out = [("up", 0, 0, 0, 0, 0), ("router",)]
    for i in range(2 * NS):
        rows = (0, 0, 0)
        for g, first in MAX_AT.items():
            if head and first <= i < first + MAX_HALVES:
                rows = (g, (i - first) * MAX0 // MAX_HALVES, (i - first + 1) * MAX0 // MAX_HALVES)
        if i + 1 < 2 * NS:
            out.append(("up", (i + 1) // 2, (i + 1) % 2, *rows))
        out.append(("down", i // 2, i % 2))
        if i == 1:
            out.append(("rank",))
        if head:
            out += HEAD_AT.get(i, [])
    return out


def step_max(n, u, part):
    for g, (n0, n1) in STEP_MAX.items():
        if n0 <= n < n1:
            at, end = 3 * ((n - n0) * UNITS + u) + part, 3 * ((n1 - n0) * UNITS - 2)
            return g, MAX0 * min(at, end) // end, MAX0 * min(at + 1, end) // end
    return 0, 0, 0


HEAD_USES = [("turn", 0), ("turn", 1), ("qk", 0), ("qk", 1), ("qk", 2), ("qk", 3), ("v", 0), ("v", 1)]


def psum_uses(head):
    st, s1 = [], []
    for n in range(STEPS):
        for u in range(UNITS):
            st.append(("att", n, u))
            for part in range(3):
                g, i0, i1 = step_max(n, u, part)
                s1 += [("max", g, i) for i in range(i0, i1)]
    st += [(kind, h) for kind in ("ot", "op", "ln") for h in range(2)]
    for kind, *at in moves(head):
        if kind == "up":
            st += [("ffn", at[0], 2 * at[1]), ("ffn", at[0], 2 * at[1] + 1)]
            s1 += [("max", at[2], i) for i in range(at[3], at[4])]
        elif kind == "down":
            s1 += [("down", at[0], at[1], t) for t in range(4)]
        elif kind in ("turn", "qk", "v"):
            st.append((kind, at[0]))
    return st, s1


ST_ORDER, S1_ORDER = {h: psum_uses(h)[0] for h in (True, False)}, {h: psum_uses(h)[1] for h in (True, False)}
ST_AT = {h: {use: i for i, use in enumerate(ST_ORDER[h])} for h in ST_ORDER}
S1_AT = {h: {use: i for i, use in enumerate(S1_ORDER[h])} for h in S1_ORDER}
ST_USES, S1_USES = len(ST_ORDER[True]), len(S1_ORDER[True])
ST_HEAD = len(HEAD_USES)
S1_SETUP = 4
S1_HEAD = S1_SETUP + HEAD_MAX * MAX0
MISC = ["out0", "max1", "out1", "out2", "out3", "max2", "out4", "out5", "out6", "max3",
        "out7", "out8", "out9", "out10", "out11", "router", "rank", "max0"]
MISC_AT = {name: i for i, name in enumerate(MISC)}
MISC_USES = len(MISC)
MASKS = sum(len(d) for d in DIAG) * GH * NG
DVE_STEPS = 72
DVE_SETUP = 26
POOL_SET = 12 + 2 * NE


def adaln_layer(nc, x, w_qk, w_v, w_o, ffn_w, router_w, bias, c_t, w_mod, out):
    assert ST_USES % 2 == 0 and S1_USES % 2 == 0 and ST_HEAD % 2 == 0 and S1_HEAD % 2 == 0 and STEPS % 2 == 0
    gates_dram = nc.dram_tensor("gates", [B, 4 * D], F32).ap()
    part_dram = nc.dram_tensor("part", [B, T, D], F32).ap()
    list_dram = nc.dram_tensor("lists", [NE * LIST + ROWS, D], F32).ap()
    routed_dram = nc.dram_tensor("routed", [TILES * ROWS, D], F32).ap()
    ffn_parts = nc.dram_tensor("ffn_parts", [NU, P, 2 * UW], F16).ap()
    x_v = x.rearrange("b (t p) d -> b p t d", p=P)
    part_v = part_dram.rearrange("b (t p) d -> b p t d", p=P)
    out_v = out.rearrange("b (t p) d -> b p t d", p=P)

    with ExitStack() as ctx:
        def sb(name, shape, dt):
            return ctx.enter_context(nc.sbuf_tensor(name, shape, dt))

        def psum(name, shape, dt):
            return ctx.enter_context(nc.psum_tensor(name, shape, dt))

        def sem(name):
            return ctx.enter_context(nc.semaphore(name))

        probs = sb("probs", [P, 2, GH * PTW], F32)
        q_stack = sb("q_stack", [P, NG, GH, T], BF16)
        k_stack = sb("k_stack", [P, NG, GH, T], BF16)
        x_sb = sb("x_sb", [P, NT, D], F32)
        norm = sb("norm", [P, NT, D], F32)
        feat = sb("feat", [P, NF, T], F32)
        v_sb = sb("v_sb", [P, NT, NH * VW + 16], F32)
        o_tok = sb("o_tok", [P, NT, D], F32)
        small = sb("small", [P, 1024], F32)
        wqk_sb = sb("wqk_sb", [P, NG, NF, P], F32)
        wv_sb = sb("wv_sb", [P, NF, D], F32)
        wo_sb = sb("wo_sb", [P, NF, D], F32)
        rw_sb = sb("rw_sb", [P, NF, NE], F32)
        ffn_sb = sb("ffn_sb", [P, 2, 2, UW], F16)
        shift_rows = sb("shift_rows", [SHIFT * GH, T], BF16)
        gates = sb("gates_sb", [P, 4, D], F32)
        mask = sb("mask", [P, 512], BF16)
        junk = sb("junk", [P, 2, 512], BF16)
        ident = sb("ident", [P, P], F32)
        ident_b = sb("ident_b", [P, P], BF16)
        max_part = sb("max_part", [P, GH, NT + 4], F32)
        max_bf = sb("max_bf", [P, NT, SHIFT, GH], BF16)
        l_inv = sb("l_inv", [P, 4 * GH], F32)
        stats = sb("stats", [P, NT, 6], F32)
        mean_var = sb("mean_var", [P, NT, 2], F32)
        rstd = sb("rstd", [P, 3, NT], F32)
        mod_t = sb("mod_t", [P, B, 8], F32)
        mod_col = sb("mod_col", [P, 2, 4], F32)
        bias_sb = sb("bias_sb", [P, NE], F32)
        desc = sb("desc", [P, NE], F32)
        score = sb("score", [P, NT, NE], F32)
        choice = sb("choice", [P, NT, NE], F32)
        hot = sb("hot", [P, 2, NT, NE], F32)
        peak = sb("peak", [P, NT], F32)
        tri = sb("tri", [P, P], BF16)
        ones = sb("ones", [P, P], BF16)
        chosen = sb("chosen", [P, NT, NE], BF16)
        before = sb("before", [P, NT + 1, NE], BF16)
        list_at = sb("list_at", [P, NE], F32)
        slot = sb("slot", [P, NT, NE], F32)
        picks = sb("picks", [P, TOPK, NT, NE], F32)
        slot_f = sb("slot_f", [P, TOPK * NT], F32)
        slot_now = sb("slot_now", [P, 2, TOPK, NT], U32)
        slot_all = sb("slot_all", [P, B, TOPK * NT], F32)
        gate_all = sb("gate_all", [P, B, TOPK * NT], F32)
        table = sb("table", [P, 2, TILES], I32)
        tails = sb("tails", [P, NE], I32)
        tile_i = sb("tile_i", [P, TILES], I32)
        eps = sb("eps", [P, 1], F32)

        listed = q_stack[:, NG - 1, :, :].rearrange("p j n -> p (j n)").bitcast(F32).rearrange("p (t d) -> p t d", d=D)
        wmod_sb = probs[:, 0, 0:NF * 6 * D].rearrange("p (f n) -> p f n", f=NF)
        mod_sb = probs[0:B, 0, 4096:4096 + 6 * D]
        guard = probs[0:B, 0, 6144:6144 + 4 * D].rearrange("p (a m n) -> p a m n", a=2, m=2)
        ct_sb = feat[:, 0, 0:NF * B]
        silu_c = feat[:, 1, 0:NF * B].rearrange("p (f b) -> p f b", f=NF)
        parts = [probs[:, 0, g * 1536:(g + 1) * 1536].bitcast(BF16).rearrange("p (a n) -> p a n", a=3) for g in range(NG)]
        rest = [probs[:, 0, 6 * T:7 * T], probs[:, 1, 0:T]]
        x1 = probs[:, 1, T:3 * T].rearrange("p (t d) -> p t d", t=NT)
        feat1 = probs[:, 1, 3 * T:5 * T].rearrange("p (f n) -> p f n", f=NF)
        feat_parts = probs[:, 1, 5 * T:7 * T].bitcast(F16).rearrange("p (a f n) -> p a f n", a=2, f=NF)
        o_raw = small[:, 0:512]
        silu_h = small[:, :].rearrange("p (a n) -> p a n", a=2)
        hidden = o_tok[:, :, :].rearrange("p t d -> p (t d)").bitcast(F16).rearrange("p (c a h n) -> p c a h n", c=2, a=2, h=2)
        stage = [buf[:, :, :].rearrange("p t d -> p (t d)")[:, 0:UW] for buf in (o_tok, norm)]
        w_slot = [ffn_sb[:, s, :, :] for s in range(2)]
        w_slot += [probs[:, 0, s * UW:(s + 1) * UW].bitcast(F16).rearrange("p (a n) -> p a n", a=2) for s in range(2)]
        w_up = [[w[:, a, 0:NF * 2 * RH].rearrange("p (f n) -> p f n", f=NF) for a in range(2)] for w in w_slot]
        w_down = [[w[:, a, NF * 2 * RH:].rearrange("p (h n) -> p h n", h=2) for a in range(2)] for w in w_slot]
        tile_in = [x_sb[:, 4 * c:4 * c + 4, :] for c in range(2)]
        tile_out = [norm[:, 4 * c:4 * c + 4, :] for c in range(2)]
        flat = probs[:, :, :].rearrange("p a n -> p (a n)")
        picked = [[flat[:, (2 * c + r) * 2 * T:(2 * c + r + 1) * 2 * T].rearrange("p (t d) -> p t d", d=D) for r in range(TOPK)] for c in range(2)]
        part_x = [flat[:, (8 + 2 * c) * T:(10 + 2 * c) * T].rearrange("p (t d) -> p t d", d=D) for c in range(2)]
        part_g = [flat[:, 12 * T + c * D:12 * T + (c + 1) * D] for c in range(2)]

        st = [psum(f"st{i}", [P, 1024], F32) for i in range(2)]
        s1 = [psum(f"s1_{i}", [P, 512], F32) for i in range(2)]
        pv = psum("pv", [P, 512], F32)
        misc = psum("misc", [P, 512], F32)
        misc_b = misc[:, :].bitcast(BF16)

        weights_in, pool_set = sem("weights_in"), sem("pool_set")
        x_in, x1_in, gates_in, out_done = sem("x_in"), sem("x1_in"), sem("gates_in"), sem("out_done")
        w_high, w_low = sem("w_high"), sem("w_low")
        w_stored = [sem(f"w_stored{s}") for s in range(2)]
        stage_in = [sem(f"stage_in{s}") for s in range(2)]
        ffn_in = [sem(f"ffn_in{s}") for s in range(2)]
        stacked = [sem(f"stacked{g}") for g in range(NG)]
        shift_in = sem("shift_in")
        st_full, s1_full, pv_full, misc_full = sem("st_full"), sem("s1_full"), sem("pv_full"), sem("misc_full")
        s1_free, scaled = sem("s1_free"), sem("scaled")
        dve_step, waits_apart = sem("dve_step"), sem("waits_apart")
        var_ready, std_ready = sem("var_ready"), sem("std_ready")
        norm1_ready, norm2_ready = sem("norm1_ready"), sem("norm2_ready")
        mod1_ready, mod2_ready = sem("mod1_ready"), sem("mod2_ready")
        feat_ready, feat1_ready = sem("feat_ready"), sem("feat1_ready")
        feat_high, feat_low = sem("feat_high"), sem("feat_low")
        part0_ready, rest_ready, part1_ready, part2_ready = sem("part0"), sem("rest"), sem("part1"), sem("part2")
        v_ready, max_ready, rows_ready = sem("v_ready"), sem("max_ready"), sem("rows_ready")
        exp_done, masked = sem("exp_done"), sem("masked")
        raw_ready, o_ready = sem("raw_ready"), sem("o_ready")
        score_ready = sem("score_ready")
        silu_ready, hidden_ready, hidden_high, hidden_low = sem("silu"), sem("hidden_ready"), sem("hidden_high"), sem("hidden_low")
        out_scaled, out_ready = sem("out_scaled"), sem("out_ready")
        c_ready, guard_ready = sem("c_ready"), sem("guard_ready")
        list_scaled, list_ready, listed_done = sem("list_scaled"), sem("list_ready"), sem("listed_done")
        chosen_ready, slots_ready = sem("chosen_ready"), sem("slots_ready")
        table_ready, zeros_done = sem("table_ready"), sem("zeros_done")
        rows_in, w_in = [sem(f"rows_in{c}") for c in range(2)], [sem(f"w_in{s}") for s in range(WSLOTS)]
        turned, high_ready, low_ready = sem("turned"), sem("high_ready"), sem("low_ready")
        up_full, y_full, y_free = sem("up_full"), sem("y_full"), sem("y_free")
        y_done = [sem(f"y_done{c}") for c in range(2)]
        pick_ready, sum_step, sum_ready = sem("pick_ready"), sem("sum_step"), sem("sum_ready")
        picked_in, part_in, sum_done = ([sem(f"{n}{c}") for c in range(2)] for n in ("picked_in", "part_in", "sum_done"))

        block = ctx.enter_context(nc.Block())

        def apart(engine):
            engine.sem_inc(waits_apart, 1)

        def st_at(b, head, use):
            return ST_HEAD + b * ST_USES + ST_AT[head][use]

        def s1_at(b, head, use):
            return S1_HEAD + b * S1_USES + S1_AT[head][use]

        def hidden_at(b, u, k):
            return b * (NS * 4) + u * 4 + k

        def routed_at(i, k):
            return B * (NS * 4) + i * 2 + k

        def misc_at(b, name):
            return HEAD_MAX + b * MISC_USES + MISC_AT[name]

        def head_st(b, use):
            return HEAD_USES.index(use) if isinstance(b, int) and b == 0 else st_at(b - 1, True, use)

        def head_max(b, g, i):
            return S1_SETUP + g * MAX0 + i if isinstance(b, int) and b == 0 else s1_at(b - 1, True, ("max", g, i))

        STACK = 16 * 2 * len(Q_PART)
        LISTED = 16 * TOPK * NT

        @block.sync
        def _(sp):
            loads = ((ct_sb, c_t), (wmod_sb, w_mod), (wqk_sb[:, :, :, :], w_qk), (wv_sb[:, :, :], w_v),
                     (wo_sb[:, :, :], w_o), (rw_sb[:, :, :], router_w), (bias_sb[:, :], bias))

            def load_x1(b):
                sp.dma_start(x1, x_v[bass.ds(b, 1)].rearrange("o p t d -> (o p) t d")).then_inc(x1_in, 16)

            def stack(b, g):
                sp.wait_ge(part2_ready, b * NG + (g + 1))
                for i in range(len(Q_PART)):
                    rows = slice(HD * i, HD * i + HD)
                    sp.dma_start(q_stack[rows, g, :, :], parts[g][0:64, Q_PART[i], :]).then_inc(stacked[g], 16)
                    sp.dma_start(k_stack[rows, g, :, :], parts[g][64:128, K_PART[i], :]).then_inc(stacked[g], 16)

            def shift(b, g):
                sp.wait_ge(rows_ready, b * NG + (g + 1))
                sp.dma_start(q_stack[KS:KS + SHIFT, g, :, :], shift_rows[:, :]).then_inc(shift_in, 16)

            def load_unit(u, s):
                sp.dma_start(ffn_sb[:, s, :, :], ffn_parts[bass.ds(u, 1)].rearrange("o p n -> (o p) n")).then_inc(ffn_in[s], 16)

            def rows_of(dram, row):
                return dram[bass.ds(row, ROWS), :].rearrange("(t p) d -> p t d", p=P)

            def batch(b, head):
                sp.wait_ge(out_ready, b * 2 + 1)
                sp.dma_start(x_sb[:, :, :], x_v[bass.ds(b, 1)].rearrange("o p t d -> (o p) t d")).then_inc(x_in, 16)
                sp.dma_start(gates[:, :, :].rearrange("p m n -> p (m n)"),
                             gates_dram[bass.ds(b, 1), :].to_broadcast([P, 4 * D])).then_inc(gates_in, 16)
                load_unit(0, 0)
                sp.wait_ge(out_done, (b + 1) * 16)
                sp.dma_start(stage[1], ffn_w[bass.ds(b + NS, 1)].rearrange("o p n -> (o p) n")).then_inc(stage_in[1], 16)
                for g in STEP_MAX:
                    shift(b, g)
                sp.wait_ge(w_low, b + (NS + 1))
                apart(sp)
                sp.dma_start(ffn_parts[bass.ds(b + NS, 1)].rearrange("o p n -> (o p) n"), ffn_sb[:, 1, :, :].rearrange("p a n -> p (a n)")).then_inc(w_stored[1], 16)
                sp.wait_ge(w_stored[1], b * 16 + (NS // 2 + 1) * 16)
                apart(sp)
                load_unit(1, 1)
                if head:
                    sp.wait_ge(pv_full, (b + 1) * STEPS)
                    load_x1(b + 1)
                for u in range(2, NS):
                    sp.wait_ge(s1_free, s1_at(b, head, ("down", u - 2, 1, 3)) + 1)
                    load_unit(u, u % 2)
                    if u == 2 and head:
                        for g in range(NG - 1):
                            stack(b + 1, g)
                if head:
                    shift(b + 1, 0)
                    sp.wait_ge(listed_done, (b + 1) * LISTED)
                    apart(sp)
                    stack(b + 1, NG - 1)
                else:
                    sp.wait_ge(table_ready, 1)
                    for e in range(NE):
                        row = sp.value_load(tails[0:1, e:e + 1], min_val=e * LIST, max_val=e * LIST + B * T)
                        sp.dma_start(rows_of(list_dram, row), x1[:, 0:4, :]).then_inc(zeros_done, 16)
                    sp.dma_start(rows_of(list_dram, NE * LIST), x1[:, 0:4, :]).then_inc(zeros_done, 16)
                sp.wait_ge(out_ready, b * 2 + 3)
                sp.dma_start(part_v[bass.ds(b, 1)].rearrange("o p t d -> (o p) t d"), norm[:, :, :]).then_inc(out_done, 16)

            for dst, src in loads:
                sp.dma_start(dst, src).then_inc(weights_in, 16)
            load_x1(0)
            for u in range(2):
                sp.dma_start(stage[u], ffn_w[u]).then_inc(stage_in[u], 16)
            sp.wait_ge(guard_ready, 1)
            sp.dma_start(gates_dram, guard[:, :, :, :]).then_inc(out_done, 16)
            sp.wait_ge(out_done, 16)
            for g in range(NG):
                stack(0, g)
            for u in range(NS):
                if u == 0:
                    shift(0, 0)
                sp.wait_ge(w_low, u + 1)
                sp.dma_start(ffn_parts[u], ffn_sb[:, u % 2, :, :].rearrange("p a n -> p (a n)")).then_inc(w_stored[u % 2], 16)
                if u + 2 < NS:
                    sp.dma_start(stage[u % 2], ffn_w[u + 2]).then_inc(stage_in[u % 2], 16)
            for s in range(2):
                sp.wait_ge(w_stored[s], 16 * (NS // 2))
            with sp.Fori(0, B - 1) as b:
                batch(b, True)
            batch(B - 1, False)

            sp.wait_ge(listed_done, B * LISTED)
            sp.wait_ge(zeros_done, 16 * (NE + 1))
            sp.wait_ge(out_done, 16 * (B + 1))

            def first_row(i):
                return sp.value_load(table[0:1, 0, bass.ds(i, 1)], min_val=0, max_val=NE * LIST)

            def load_tile(i, s, first):
                if not first:
                    sp.wait_ge(turned, i - 1)
                    apart(sp)
                sp.dma_start(tile_in[s % 2], rows_of(list_dram, first_row(i))).then_inc(rows_in[s % 2], 16)
                if not first:
                    sp.wait_ge(y_free, i * 4 - (4 * WSLOTS - 6))
                    apart(sp)
                e = sp.value_load(table[0:1, 1, bass.ds(i, 1)], min_val=0, max_val=NE - 1)
                sp.dma_start(w_slot[s].rearrange("p a n -> p (a n)"), ffn_parts[bass.ds(e + NS, 1)].rearrange("o p n -> (o p) n")).then_inc(w_in[s], 16)

            def store_tile(i, s):
                sp.wait_ge(y_free, i * 4 + 6)
                apart(sp)
                sp.dma_start(rows_of(routed_dram, i * ROWS), tile_out[s % 2]).then_inc(y_done[s % 2], 16)

            for i in range(2):
                load_tile(i, i, True)
            for i in range(2, WSLOTS):
                sp.wait_ge(turned, i - 1)
                load_tile(i, i, True)
                store_tile(i - 2, i)
            with sp.Fori(1, TILES // WSLOTS) as quad:
                for s in range(WSLOTS):
                    load_tile(quad * WSLOTS + s, s, False)
                    store_tile(quad * WSLOTS + (s - 2), s)
            for i in range(TILES - 2, TILES):
                store_tile(i, i)
            for c in range(2):
                sp.wait_ge(y_done[c], 16 * (TILES // 2 + 1))

            def load_part(b, c):
                sp.dma_start(part_x[c], part_v[bass.ds(b, 1)].rearrange("o p t d -> (o p) t d")).then_inc(part_in[c], 16)
                sp.dma_start(part_g[c], gates_dram[bass.ds(b, 1), D:2 * D].to_broadcast([P, D])).then_inc(part_in[c], 16)

            for b in range(2):
                load_part(b, b)
            with sp.Fori(0, B // 2 - 1) as pair:
                for c in range(2):
                    sp.wait_ge(sum_ready, pair * 2 + (c + 1))
                    apart(sp)
                    sp.dma_start(out_v[bass.ds(pair * 2 + c, 1)].rearrange("o p t d -> (o p) t d"), picked[c][0]).then_inc(sum_done[c], 16)
                    load_part(pair * 2 + (c + 2), c)
            for c in range(2):
                sp.wait_ge(sum_ready, B - 1 + c)
                sp.dma_start(out_v[B - 2 + c], picked[c][0]).then_inc(sum_done[c], 16)
            for c in range(2):
                sp.wait_ge(sum_done[c], 16 * (B // 2))

        @block.gpsimd
        def _(pool):
            gp = nc.gpsimd
            gp.memset(ident[:, :], 0.0).then_inc(pool_set, 1)
            gp.memset(mask[:, :], 0.0).then_inc(pool_set, 1)
            gp.memset(v_sb[:, :, :], 1.0).then_inc(pool_set, 1)
            gp.memset(eps[:, :], EPS).then_inc(pool_set, 1)
            for e in range(NE):
                gp.memset(desc[:, e:e + 1], float(NE - e)).then_inc(pool_set, 1)
            gp.memset(tri[:, :], 1.0).then_inc(pool_set, 1)
            gp.memset(ones[:, :], 1.0).then_inc(pool_set, 1)
            gp.memset(before[:, :, :], 0.0).then_inc(pool_set, 1)
            for e in range(NE):
                gp.memset(list_at[:, e:e + 1], float(e * LIST)).then_inc(pool_set, 1)
            gp.iota(tile_i[:, :], [[1, TILES]], 0, 0).then_inc(pool_set, 1)
            pool.wait_ge(pool_set, 8 + 2 * NE)
            gp.affine_select(tri[:, :], tri[:, :], [[1, P]], ALU.is_ge, 0.0, -1, -1).then_inc(pool_set, 1)
            gp.affine_select(ident[:, :], ident[:, :], [[-1, P]], ALU.not_equal, 1.0, 0, 1).then_inc(pool_set, 1)
            gp.affine_select(mask[:, 384:512], mask[:, 384:512], [[-1, P]], ALU.is_ge, NEG, 0, 1).then_inc(pool_set, 1)
            pool.wait_ge(pool_set, 11 + 2 * NE)
            gp.tensor_copy(ident_b[:, :], ident[:, :]).then_inc(pool_set, 1)

            def part2(b, g):
                pool.wait_ge(part1_ready, b * NG + (g + 1))
                gp.tensor_tensor(parts[g][:, 2, :], rest[g % 2], parts[g][:, 1, :], ALU.subtract).then_inc(part2_ready, 1)

            def low(b, u, k):
                pool.wait_ge(hidden_high, hidden_at(b, u, k + 1))
                gp.tensor_tensor(hidden[:, k // 2, 1, k % 2, :], silu_h[:, k % 2, :], hidden[:, k // 2, 0, k % 2, :],
                                 ALU.subtract).then_inc(hidden_low, 1)

            def batch(b, head):
                for n in range(STEPS):
                    c = n % NC
                    for j in range(GH):
                        pool.wait_ge(exp_done, b * STEPS * UNITS + (n * UNITS + 2 * j + 2))
                        apart(pool)
                        row = probs[:, n % 2, j * PTW:(j + 1) * PTW]
                        for at, step, k in DIAG[c]:
                            v = row[:, at:at + step * (k - 1) + P].rearrange("p (m n) -> p m n", n=P)[:, 0::step // P, :]
                            gp.affine_select(v, v, [[0, k], [1, P]], ALU.is_ge, 0.0, 0, -1).then_inc(masked, 1)
                pool.wait_ge(norm2_ready, (b + 1) * NT)
                gp.tensor_tensor(listed, norm[:, :, :], gates[:, 3, :].unsqueeze(1).to_broadcast([P, NT, D]), ALU.mult).then_inc(list_scaled, 1)
                pool.wait_ge(list_scaled, b + 1)
                gp.tensor_tensor(listed, listed, gates[:, 2, :].unsqueeze(1).to_broadcast([P, NT, D]), ALU.add).then_inc(list_ready, 1)
                halves = 0
                for kind, *at in moves(head):
                    if kind == "up":
                        for k in range(2):
                            low(b, at[0], 2 * at[1] + k)
                        halves += 1
                        if halves == 4:
                            pool.wait_ge(slots_ready, b + 1)
                            apart(pool)
                            pool.wait_ge(list_ready, b + 1)
                            apart(pool)
                        if halves >= 4:
                            for n in range(4 * (halves - 4), min(TOPK * NT, 4 * (halves - 3))):
                                gp.indirect_dma_start(list_dram, bass.IndirectOffsetOnAxis(ap=slot_now[:, 0, n % TOPK, n // TOPK:n // TOPK + 1], axis=0),
                                                      listed[:, n // TOPK, :], None).then_inc(listed_done, 16)
                    elif kind == "qk":
                        part2(b + 1, at[0])
                pool.wait_ge(s1_free, s1_at(b, head, ("down", NS - 1, 1, 3)) + 1)
                gp.tensor_tensor(norm[:, 4:8, :], norm[:, 4:8, :], gates[:, 1, :].unsqueeze(1).to_broadcast([P, 4, D]),
                                 ALU.mult).then_inc(out_scaled, 1)
                pool.wait_ge(out_scaled, b + 1)
                gp.tensor_tensor(norm[:, 4:8, :], norm[:, 4:8, :], x_sb[:, 4:8, :], ALU.add).then_inc(out_ready, 1)

            for _ in range(2):
                pool.sem_inc(hidden_low, 1)
            for g in range(NG):
                part2(0, g)
            with pool.Fori(0, B - 1) as b:
                batch(b, True)
            batch(B - 1, False)

            with pool.Fori(0, TILES // 2) as pair:
                for c in range(2):
                    for h in range(2):
                        pool.wait_ge(hidden_high, routed_at(pair * 2 + c, h + 1))
                        gp.tensor_tensor(hidden[:, c, 1, h, :], silu_h[:, h, :], hidden[:, c, 0, h, :], ALU.subtract).then_inc(hidden_low, 1)
            for c in range(2):
                pool.wait_ge(y_done[c], 16 * (TILES // 2 + 1))
            with pool.Fori(0, B // 2) as pair:
                for c in range(2):
                    pool.wait_ge(pick_ready, pair * 2 + (c + 1))
                    apart(pool)
                    for n in range(TOPK * NT):
                        r, t = n // NT, n % NT
                        gp.indirect_dma_start(picked[c][r][:, t, :], None, routed_dram,
                                              bass.IndirectOffsetOnAxis(ap=slot_now[:, c, r, t:t + 1], axis=0)).then_inc(picked_in[c], 16)

        @block.scalar
        def _(act):
            sc = nc.scalar
            act.wait_ge(weights_in, 16 * 7)
            sc.activation(silu_c.rearrange("p f b -> p (f b)"), ct_sb, ACT.Silu).then_inc(c_ready, 1)
            act.wait_ge(pool_set, POOL_SET)

            def norm_std(order, t0=0, t1=NT):
                act.wait_ge(var_ready, order)
                sc.activation(rstd[:, 0, t0:t1], mean_var[:, t0:t1, 1], ACT.Sqrt, bias=eps[:, 0:1]).then_inc(std_ready, 1)

            def modulate(to, src, k, f, done):
                sc.activation(to, src, ACT.Identity, bias=mod_col[:, k, f:f + 1],
                                     scale=mod_col[:, k, 2 + f:3 + f]).then_inc(done, 1)

            def turn1(b, f):
                at = head_st(b, ("turn", f))
                act.wait_ge(st_full, at + 1)
                modulate(feat1[:, f, :], st[HEAD_USES.index(("turn", f)) % 2][:, :], 0, f, feat1_ready)

            def part0(b, g):
                act.wait_ge(st_full, head_st(b, ("qk", g)) + 1)
                sc.activation(parts[g][:, 0, :], st[HEAD_USES.index(("qk", g)) % 2][:, :], ACT.Copy).then_inc(part0_ready, 1)

            def part1(b, g):
                act.wait_ge(rest_ready, b * NG + (g + 1))
                sc.activation(parts[g][:, 1, :], rest[g % 2], ACT.Copy).then_inc(part1_ready, 1)

            def shift_copy(b, g, count):
                act.wait_ge(misc_full, count)
                if g >= 1 or not (isinstance(b, int) and b == 0):
                    act.wait_ge(shift_in, b * (NG * 16) + g * 16)
                sc.activation(shift_rows[:, :], misc_b[0:SHIFT * GH, :], ACT.Copy).then_inc(rows_ready, 1)

            def raw_copy(b, n):
                nq = CHUNKS[n % NC][1]
                act.wait_ge(pv_full, b * STEPS + (n + 1))
                if n >= 1:
                    act.wait_ge(misc_full, misc_at(b, f"out{n - 1}") + 1)
                sc.activation(o_raw[:, 0:nq], pv[:, 0:nq], ACT.Copy).then_inc(raw_ready, 1)

            def exps(b, head, n, u):
                c, j, t = n % NC, u // 2, u % 2
                w = (1024, CHUNKS[c][3] - 1024)[t]
                act.wait_ge(st_full, st_at(b, head, ("att", n, u)) + 1)
                at = j * PTW + 1024 * t
                sc.activation(probs[:, n % 2, at:at + w], st[u % 2][:, 0:w], ACT.Exp, scale=SCALE).then_inc(exp_done, 1)

            def hide(b, u, c, full):
                for k in (2 * c, 2 * c + 1):
                    act.wait_ge(st_full, full(k) + 1)
                    act.wait_ge(hidden_low, hidden_at(b, u, k + 1))
                    sc.activation(silu_h[:, k % 2, :], st[k % 2][:, 0:512], ACT.Silu, scale=1.0 / W_SCALE).then_inc(silu_ready, 1)
                for k in (2 * c, 2 * c + 1):
                    act.wait_ge(hidden_ready, hidden_at(b, u, k + 3))
                    sc.activation(hidden[:, c, 0, k % 2, :], silu_h[:, k % 2, :], ACT.Copy).then_inc(hidden_high, 1)

            def batch(b, head):
                for n in range(STEPS):
                    if n >= 2:
                        act.wait_ge(pv_full, b * STEPS + (n - 1))
                    for u in range(UNITS):
                        for g in range(NG):
                            if n == 0 and u % 2 == 0 and g * 3 * T // 2 // PTW == u // 2:
                                act.wait_ge(stacked[g], (b + 1) * STACK)
                        exps(b, head, n, u)
                    if n >= 1:
                        raw_copy(b, n - 1)
                    if n == STEPS - NC:
                        act.wait_ge(stage_in[1], b * 16 + (NS // 2 + 1) * 16)
                        sc.activation(ffn_sb[:, 1, 0, :], stage[1], ACT.Copy, scale=W_SCALE).then_inc(w_high, 1)
                    for g, (_, n1) in STEP_MAX.items():
                        if n == n1 - 1:
                            shift_copy(b, g, misc_at(b, f"max{g}") + 1)
                raw_copy(b, STEPS - 1)
                for f in range(NF):
                    act.wait_ge(st_full, st_at(b, head, ("ot", f)) + 1)
                    sc.activation(feat[:, f, :], st[ST_AT[head][("ot", f)] % 2][:, :], ACT.Copy).then_inc(feat_ready, 1)
                act.wait_ge(mod2_ready, b + 1)
                for h in range(2):
                    norm_std(b * 3 + (2 + h), 4 * h, 4 * h + 4)
                    act.wait_ge(st_full, st_at(b, head, ("ln", h)) + 1)
                    tokens = slice(512 * h, 512 * h + 512)
                    for f in range(NF):
                        modulate(feat[:, f, tokens], st[ST_AT[head][("ln", h)] % 2][:, 512 * f:512 * f + 512], 1, f, feat_ready)
                    act.wait_ge(feat_ready, b * 3 * NF + (h + 2) * NF)
                    sc.activation(feat_parts[:, 0, :, tokens], feat[:, :, tokens], ACT.Copy).then_inc(feat_high, 1)
                for kind, *at in moves(head):
                    if kind == "up":
                        hide(b, at[0], at[1], lambda k: st_at(b, head, ("ffn", at[0], k)))
                    elif kind == "router":
                        if head:
                            norm_std(b * 3 + 4)
                            act.wait_ge(mod1_ready, b + 2)
                        act.wait_ge(misc_full, misc_at(b, "router") + 1)
                        sc.activation(score[:, :, :].rearrange("p t e -> p (t e)"), misc[:, 0:NT * NE], ACT.Sigmoid).then_inc(score_ready, 1)
                    elif kind == "max_turn":
                        shift_copy(b + 1, at[0], misc_at(b, f"max{at[0]}") + 1)
                    elif kind == "turn":
                        turn1(b + 1, at[0])
                    elif kind == "qk":
                        part0(b + 1, at[0])
                        if at[0] >= 1:
                            part1(b + 1, at[0] - 1)
                        if at[0] == NG - 1:
                            part1(b + 1, at[0])

            norm_std(1)
            act.wait_ge(mod1_ready, 1)
            act.wait_ge(out_done, 16)
            for f in range(NF):
                turn1(0, f)
            for g in range(NG + 1):
                if g < NG:
                    part0(0, g)
                if g >= 1:
                    part1(0, g - 1)
            for u in range(NS):
                if u == 2:
                    shift_copy(0, 0, 1)
                act.wait_ge(stage_in[u % 2], 16 * (u // 2 + 1))
                if u >= 2:
                    act.wait_ge(w_stored[u % 2], 16 * (u // 2))
                sc.activation(ffn_sb[:, u % 2, 0, :], stage[u % 2], ACT.Copy, scale=W_SCALE).then_inc(w_high, 1)
            with act.Fori(0, B - 1) as b:
                batch(b, True)
            batch(B - 1, False)

            def high(i, c):
                act.wait_ge(turned, i + 1)
                for f in range(NF):
                    last = sc.activation(feat_parts[:, 0, f, 512 * c:512 * c + 512], (pv, misc)[f][:, :], ACT.Copy)
                last.then_inc(high_ready, 1)

            def routed(i, c, ahead=None):
                for h in range(2):
                    act.wait_ge(up_full, i * 2 + (h + 1))
                    act.wait_ge(hidden_low, routed_at(i, h + 1))
                    sc.activation(silu_h[:, h, :], st[h][:, 0:512], ACT.Silu, scale=1.0 / W_SCALE).then_inc(silu_ready, 1)
                if ahead is not None:
                    high(*ahead)
                for h in range(2):
                    act.wait_ge(hidden_ready, routed_at(i, h + 3))
                    sc.activation(hidden[:, c, 0, h, :], silu_h[:, h, :], ACT.Copy).then_inc(hidden_high, 1)

            high(0, 0)
            high(1, 1)
            routed(0, 0)
            with act.Fori(0, TILES // 2 - 1) as pair:
                for c in range(2):
                    routed(pair * 2 + (c + 1), 1 - c, (pair * 2 + (c + 2), c))
            routed(TILES - 1, 1)

        @block.vector
        def _(dve):
            vec = nc.vector
            count = [0]

            def chain(ins, base):
                count[0] += 1
                ins.then_inc(dve_step, 1)
                dve.wait_ge(dve_step, base + count[0])

            def spread(base, x_of, t0=0, t1=NT):
                for t in range(t0, t1):
                    vec.bn_stats(stats[:, t, :], x_of[:, t, :]).then_inc(dve_step, 1)
                    count[0] += 1
                dve.wait_ge(dve_step, base + count[0])
                apart(dve)
                for t in range(t0, t1):
                    ins = vec.bn_aggr(mean_var[:, t, :], stats[:, t, :])
                ins.then_inc(var_ready, 1)

            def normed(order, base, to, x_of, done, t0=0, t1=NT):
                dve.wait_ge(std_ready, order)
                std, inv, shift = (rstd[:, i, t0:t1] for i in range(3))
                chain(vec.reciprocal(inv, std), base)
                chain(vec.scalar_tensor_tensor(shift, mean_var[:, t0:t1, 0], -1.0, inv, ALU.mult, ALU.mult), base)
                for t in range(t0, t1):
                    vec.tensor_scalar(to[:, t, :], x_of[:, t, :], rstd[:, 1, t:t + 1], rstd[:, 2, t:t + 1],
                                      ALU.mult, ALU.add).then_inc(done, 1)

            def mod_copy(b, k, done):
                vec.tensor_copy(mod_col[:, k, :], mod_t[:, bass.ds(b, 1), 4 * k:4 * k + 4].rearrange("p o k -> p (o k)")).then_inc(done, 1)

            def split(b, g):
                dve.wait_ge(part0_ready, b * NG + (g + 1))
                if g >= 2:
                    dve.wait_ge(part2_ready, b * NG + (g - 1))
                vec.tensor_tensor(rest[g % 2], st[HEAD_USES.index(("qk", g)) % 2][:, :], parts[g][:, 0, :], ALU.subtract).then_inc(rest_ready, 1)

            def take_v(b, h):
                dve.wait_ge(st_full, head_st(b, ("v", h)) + 1)
                for t in range(4):
                    to = v_sb[:, 4 * h + t, 0:NH * VW].rearrange("p (h d) -> p h d", d=VW)[:, :, 0:HD]
                    vec.tensor_copy(to, st[h % 2][:, t * D:(t + 1) * D].rearrange("p (h d) -> p h d", d=HD)).then_inc(v_ready, 1)

            def maxima(g, i0, i1, at):
                for i in range(i0, i1):
                    j, (qt, k0, nk, masked_, col) = i // NM, MAXCH[i % NM]
                    dve.wait_ge(s1_full, at(i) + 1)
                    dve.wait_ge(s1_free, at(i) - 1)
                    tile, to = s1[i % 2], max_part[:, j, col:col + 1]
                    if masked_:
                        apart(dve)
                        vec.tensor_tensor_reduce(junk[:, i % 2, 0:nk], tile[:, 0:nk], mask[:, 512 - nk:512], 1.0, NEG,
                                                 ALU.add, ALU.max, to).then_inc(s1_free, 1)
                    else:
                        vec.tensor_reduce(to, tile[:, 0:nk], AX.X, ALU.max).then_inc(s1_free, 1)

            def shifts(b, g, last, base):
                dve.wait_ge(s1_free, last + 1)
                hi = max_part[:, :, 4:NT]
                chain(vec.tensor_tensor(hi, hi, max_part[:, :, NT:NT + 4], ALU.max), base)
                m = max_part[:, :, 0:NT]
                parts_of = [max_bf[:, :, a, :].rearrange("p t j -> p j t") for a in range(SHIFT)]
                chain(vec.tensor_scalar(parts_of[0], m, -1.0, None, ALU.mult), base)
                vec.scalar_tensor_tensor(parts_of[1], m, -1.0, parts_of[0], ALU.mult, ALU.subtract).then_inc(max_ready, 1)
                dve.wait_ge(max_ready, b * NG + (g + 1))
                if not isinstance(b, int):
                    apart(dve)

            def normalise(b, n, base):
                c = n % NC
                q0, nq = CHUNKS[c][:2]
                k = nq // P * GH
                dve.wait_ge(misc_full, misc_at(b, f"out{n}") + 1)
                o = misc[:, 0:k * 32].rearrange("p (k n) -> p k n", k=k)
                chain(vec.reciprocal(l_inv[:, 0:k], o[:, :, HD]), base)
                h0 = n // NC * GH * HD
                to = o_tok[:, q0 // P:(q0 + nq) // P, h0:h0 + GH * HD].rearrange("p t (j d) -> p t j d", j=GH)
                vec.tensor_tensor(to, o[:, :, 0:HD].rearrange("p (t j) d -> p t j d", j=GH),
                                  l_inv[:, 0:k].rearrange("p (t j) -> p t j", j=GH).unsqueeze(3).to_broadcast([P, nq // P, GH, HD]),
                                  ALU.mult).then_inc(o_ready, 1)

            def hide(b, u, k):
                dve.wait_ge(silu_ready, hidden_at(b, u, k + 1))
                vec.scalar_tensor_tensor(silu_h[:, k % 2, :], st[k % 2][:, 512:1024], 1.0 / W_SCALE, silu_h[:, k % 2, :],
                                         ALU.mult, ALU.mult).then_inc(hidden_ready, 1)

            def add_up(u, c, t0, t1, at):
                for t in range(t0, t1):
                    dve.wait_ge(s1_full, at(t) + 1)
                    y, total = s1[t % 2][:, 0:D], norm[:, c * 4 + t, :]
                    if u == 0:
                        vec.tensor_copy(total, y).then_inc(s1_free, 1)
                    else:
                        vec.tensor_tensor(total, y, total, ALU.add).then_inc(s1_free, 1)

            def feature_low(b, h):
                dve.wait_ge(feat_high, b * 2 + (h + 1))
                tokens = slice(512 * h, 512 * h + 512)
                vec.tensor_tensor(feat_parts[:, 1, :, tokens], feat[:, :, tokens], feat_parts[:, 0, :, tokens], ALU.subtract).then_inc(feat_low, 1)

            def route(b, base):
                dve.wait_ge(score_ready, b + 1)

                def wide(a):
                    return a.unsqueeze(2).to_broadcast([P, NT, NE])

                chain(vec.tensor_tensor(choice[:, :, :], score[:, :, :], bias_sb[:, :].unsqueeze(1).to_broadcast([P, NT, NE]), ALU.add), base)
                for r in range(2):
                    chain(vec.tensor_reduce(peak[:, :], choice[:, :, :], AX.X, ALU.max), base)
                    chain(vec.tensor_tensor(hot[:, r, :, :], choice[:, :, :], wide(peak[:, :]), ALU.is_equal), base)
                    chain(vec.tensor_tensor(hot[:, r, :, :], hot[:, r, :, :], desc[:, :].unsqueeze(1).to_broadcast([P, NT, NE]), ALU.mult), base)
                    chain(vec.tensor_reduce(peak[:, :], hot[:, r, :, :], AX.X, ALU.max), base)
                    chain(vec.tensor_tensor(hot[:, r, :, :], hot[:, r, :, :], wide(peak[:, :]), ALU.is_equal), base)
                    if r == 0:
                        chain(vec.scalar_tensor_tensor(choice[:, :, :], hot[:, 0, :, :], NEG, choice[:, :, :], ALU.mult, ALU.add), base)
                chain(vec.tensor_copy(before[:, 0, :], before[:, NT, :]), base)
                chain(vec.tensor_tensor(chosen[:, :, :], hot[:, 0, :, :], hot[:, 1, :, :], ALU.add), base)
                for t in range(NT):
                    ins = vec.tensor_tensor(before[:, t + 1, :], before[:, t, :], chosen[:, t, :], ALU.add)
                    if t < NT - 1:
                        chain(ins, base)
                ins.then_inc(chosen_ready, 1)

            def place(b, base):
                dve.wait_ge(misc_full, misc_at(b, "rank") + 1)

                def both(a):
                    return a.unsqueeze(1).to_broadcast([P, TOPK, NT, NE])

                chain(vec.tensor_tensor(slot[:, :, :], misc[:, 0:NT * NE].rearrange("p (t e) -> p t e", e=NE),
                                        list_at[:, :].unsqueeze(1).to_broadcast([P, NT, NE]), ALU.add), base)
                chain(vec.tensor_tensor(picks[:, :, :, :], hot[:, :, :, :], both(slot[:, :, :]), ALU.mult), base)
                chain(vec.tensor_reduce(slot_f[:, :], picks[:, :, :, :].rearrange("p r t e -> p (r t) e"), AX.X, ALU.add), base)
                vec.tensor_copy(slot_now[:, 0, :, :].rearrange("p r t -> p (r t)"), slot_f[:, :]).then_inc(slots_ready, 1)
                chain(vec.tensor_copy(slot_all[:, bass.ds(b, 1), :].rearrange("p o n -> p (o n)"), slot_f[:, :]), base)
                chain(vec.tensor_tensor(picks[:, :, :, :], hot[:, :, :, :], both(score[:, :, :]), ALU.mult), base)
                chain(vec.tensor_reduce(gate_all[:, bass.ds(b, 1), :].rearrange("p o n -> p (o n)"),
                                        picks[:, :, :, :].rearrange("p r t e -> p (r t) e"), AX.X, ALU.add), base)

            def make_table(b, base):
                temps = probs[:, 1, 3 * T:5 * T]
                length, tiles, end = (temps[:, 8 * i:8 * i + 8] for i in range(3))
                index, which, start = (temps[:, 64 + TILES * i:64 + TILES * (i + 1)] for i in range(3))
                past = temps[:, 512:512 + TILES * NE].rearrange("p (i e) -> p i e", e=NE)

                def per_tile(a):
                    return a.unsqueeze(1).to_broadcast([P, TILES, NE])

                chain(vec.memset(x1[:, 0:4, :], 0.0), base)
                chain(vec.tensor_copy(index, tile_i[:, :]), base)
                dve.wait_ge(misc_full, misc_at(b, "max0") + 1)
                chain(vec.tensor_copy(length, misc[:, 0:NE]), base)
                chain(vec.tensor_tensor(tails[:, :], length, list_at[:, :], ALU.add), base)
                chain(vec.tensor_scalar(tiles, length, 1.0 / ROWS, 0.5 - 0.5 / ROWS, ALU.mult, ALU.add), base)
                chain(vec.tensor_scalar(tiles, tiles, float(2 ** 23), None, ALU.add), base)
                chain(vec.tensor_scalar(tiles, tiles, -float(2 ** 23), None, ALU.add), base)
                chain(vec.tensor_copy(end, tiles), base)
                for e in range(1, NE):
                    chain(vec.tensor_tensor(end[:, e:e + 1], end[:, e - 1:e], tiles[:, e:e + 1], ALU.add), base)
                chain(vec.tensor_tensor(past, index.unsqueeze(2).to_broadcast([P, TILES, NE]), per_tile(end), ALU.is_ge), base)
                chain(vec.tensor_reduce(which, past, AX.X, ALU.add), base)
                chain(vec.tensor_tensor(past, past, per_tile(tiles), ALU.mult), base)
                chain(vec.tensor_reduce(start, past, AX.X, ALU.add), base)
                chain(vec.tensor_tensor(index, index, start, ALU.subtract), base)
                chain(vec.tensor_scalar(index, index, float(ROWS), None, ALU.mult), base)
                chain(vec.scalar_tensor_tensor(index, which, float(LIST), index, ALU.mult, ALU.add), base)
                chain(vec.tensor_scalar(table[:, 0, :], index, float(NE * LIST), None, ALU.min), base)
                vec.tensor_scalar(table[:, 1, :], which, float(NE - 1), None, ALU.min).then_inc(table_ready, 1)
                every = slot_all[:, :, :].rearrange("p b n -> p (b n)")
                was, back = (temps[:, 256 + B * TOPK * NT * i:256 + B * TOPK * NT * (i + 1)] for i in range(2))
                chain(vec.tensor_scalar(end, tiles, -float(ROWS), float(LIST), ALU.mult, ALU.add), base)
                chain(vec.tensor_copy(was, every), base)
                for e in range(1, NE):
                    chain(vec.tensor_scalar(back, was, float(e * LIST), end[:, e - 1:e], ALU.is_ge, ALU.mult), base)
                    chain(vec.tensor_tensor(every, every, back, ALU.subtract), base)

            def batch(b, head):
                count[0] = 0
                base = b * DVE_STEPS + DVE_SETUP
                for n in range(STEPS):
                    for u in range(UNITS):
                        for part in range(3):
                            g, i0, i1 = step_max(n, u, part)
                            maxima(g, i0, i1, lambda i: s1_at(b, head, ("max", g, i)))
                        if u == 2 and n >= 2:
                            normalise(b, n - 2, base)
                    for g, (_, n1) in STEP_MAX.items():
                        if n == n1 - 1:
                            shifts(b, g, s1_at(b, head, ("max", g, MAX0 - 1)), base)
                dve.wait_ge(w_high, b + (NS + 1))
                vec.scalar_tensor_tensor(ffn_sb[:, 1, 1, :], stage[1], W_SCALE, ffn_sb[:, 1, 0, :], ALU.mult, ALU.subtract).then_inc(w_low, 1)
                normalise(b, STEPS - 2, base)
                mod_copy(b, 1, mod2_ready)
                normalise(b, STEPS - 1, base)
                dve.wait_ge(x_in, (b + 1) * 16)
                dve.wait_ge(gates_in, (b + 1) * 16)
                dve.wait_ge(out_done, (b + 1) * 16)
                dve.wait_ge(w_low, b + (NS + 1))
                apart(dve)
                for h in range(2):
                    dve.wait_ge(st_full, st_at(b, head, ("op", h)) + 1)
                    y = o_tok[:, 4 * h:4 * h + 4, :]
                    vec.tensor_tensor(y, st[ST_AT[head][("op", h)] % 2][:, :].rearrange("p (t d) -> p t d", d=D),
                                      gates[:, 0, :].unsqueeze(1).to_broadcast([P, 4, D]), ALU.mult).then_inc(scaled, 1)
                    dve.wait_ge(scaled, b * 2 + (h + 1))
                    if h == 1:
                        normed(b * 3 + 2, base, norm, x_sb, norm2_ready, 0, 4)
                    chain(vec.tensor_tensor(x_sb[:, 4 * h:4 * h + 4, :], x_sb[:, 4 * h:4 * h + 4, :], y, ALU.add), base)
                    spread(base, x_sb, 4 * h, 4 * h + 4)
                feature_low(b, 0)
                normed(b * 3 + 3, base, norm, x_sb, norm2_ready, 4, 8)
                feature_low(b, 1)
                if head:
                    mod_copy(b + 1, 0, mod1_ready)
                for kind, *at in moves(head):
                    if kind == "up":
                        u, c, g, i0, i1 = at
                        half = i0 + (i1 - i0) * 2 // 3
                        maxima(g, i0, half, lambda i: head_max(b + 1, g, i))
                        hide(b, u, 2 * c)
                        maxima(g, half, i1, lambda i: head_max(b + 1, g, i))
                        if u + c == 0:
                            hide(b, 0, 1)
                        if u == 0 and c == 1 and head:
                            normed(b * 3 + 4, base, x1, x1, norm1_ready)
                    elif kind == "down":
                        if at == [0, 0]:
                            dve.wait_ge(list_scaled, b + 1)
                            apart(dve)
                        last = at == [NS - 1, 1]
                        if last:
                            dve.wait_ge(s1_free, s1_at(b, head, ("down", NS - 1, 0, 3)) + 1)
                            chain(vec.tensor_tensor(norm[:, 0:4, :], norm[:, 0:4, :], gates[:, 1, :].unsqueeze(1).to_broadcast([P, 4, D]), ALU.mult), base)
                            vec.tensor_tensor(norm[:, 0:4, :], norm[:, 0:4, :], x_sb[:, 0:4, :], ALU.add).then_inc(out_ready, 1)
                        add_up(*at, 0, 2, lambda t: s1_at(b, head, ("down", *at, t)))
                        if not last:
                            hide(b, u, 2 * c + 1)
                        add_up(*at, 2, 4, lambda t: s1_at(b, head, ("down", *at, t)))
                        if at == [0, 0]:
                            route(b, base)
                        if at == [1, 0]:
                            place(b, base)
                        if at == [2, 0] and not head:
                            make_table(b, base)
                    elif kind == "router":
                        if head:
                            dve.wait_ge(x1_in, (b + 2) * 16)
                            spread(base, x1)
                    elif kind == "qk":
                        split(b + 1, at[0])
                    elif kind == "v":
                        take_v(b + 1, at[0])
                    elif kind == "shift":
                        shifts(b + 1, at[0], head_max(b + 1, at[0], MAX0 - 1), base)
                assert not head or count[0] == DVE_STEPS, count[0]

            for s in (out_ready, raw_ready, hidden_ready, hidden_ready):
                dve.sem_inc(s, 1)
            vec.memset(k_stack[KS:KS + SHIFT, :, :, :], 1.0).then_inc(dve_step, 1)
            count[0] += 1
            for k in range(3):
                dve.wait_ge(s1_full, k + 1)
                vec.tensor_copy(mod_sb[:, k * 512:(k + 1) * 512], s1[k % 2][0:B, :]).then_inc(s1_free, 1)
            dve.wait_ge(s1_free, 3)
            for m, idx in ((0, 2), (1, 5)):
                g = mod_sb[:, idx * D:(idx + 1) * D]
                chain(vec.tensor_scalar(guard[:, 0, m, :], g, 0.0, 2.0, ALU.is_ge, ALU.mult), 0)
                vec.scalar_tensor_tensor(guard[:, 1, m, :], g, -1.0, g, ALU.mult, ALU.max).then_inc(dve_step, 1)
                count[0] += 1
                chain(vec.tensor_scalar(guard[:, 0, m, :], guard[:, 0, m, :], -1.0, None, ALU.add), 0)
                ins = vec.scalar_tensor_tensor(guard[:, 0, m, :], guard[:, 1, m, :], 0.25, guard[:, 0, m, :], ALU.max, ALU.mult)
                chain(ins, 0)
            chain(vec.tensor_scalar(guard[:, 0, 1, :], guard[:, 0, 1, :], 1.0 / W_SCALE, None, ALU.mult), 0)
            chain(vec.tensor_copy(guard[:, 1, 0, :], mod_sb[:, 3 * D:4 * D]), 0)
            vec.tensor_scalar(guard[:, 1, 1, :], mod_sb[:, 4 * D:5 * D], 1.0, None, ALU.add).then_inc(guard_ready, 1)
            dve.wait_ge(s1_full, 4)
            mt = mod_t[:, :, :].rearrange("p b k -> p k b")
            ps = s1[1][:, 0:8 * B].rearrange("p (k b) -> p k b", k=8)
            for i, add in ((0, 0.0), (2, 1.0), (4, 0.0)):
                vec.tensor_scalar(mt[:, i:i + 2, :], ps[:, i:i + 2, :], add, None, ALU.add).then_inc(dve_step, 1)
                count[0] += 1
            vec.tensor_scalar(mt[:, 6:8, :], ps[:, 6:8, :], 1.0, None, ALU.add).then_inc(s1_free, 1)
            dve.wait_ge(s1_free, 4)
            mod_copy(0, 0, mod1_ready)
            dve.wait_ge(pool_set, POOL_SET)
            dve.wait_ge(x1_in, 16)
            spread(0, x1)
            normed(1, 0, x1, x1, norm1_ready)
            for g in range(NG):
                split(0, g)
            for h in range(2):
                take_v(0, h)
            for g in range(HEAD_MAX):
                maxima(g, 0, MAX0, lambda i: head_max(0, g, i))
                shifts(0, g, head_max(0, g, MAX0 - 1), 0)
            for u in range(NS):
                dve.wait_ge(w_high, u + 1)
                vec.scalar_tensor_tensor(ffn_sb[:, u % 2, 1, :], stage[u % 2], W_SCALE, ffn_sb[:, u % 2, 0, :],
                                         ALU.mult, ALU.subtract).then_inc(w_low, 1)
            assert count[0] == DVE_SETUP, count[0]
            with dve.Fori(0, B - 1) as b:
                batch(b, True)
            batch(B - 1, False)

            for _ in range(2):
                dve.sem_inc(y_free, 1)
            for c in range(2):
                dve.sem_inc(y_done[c], 16)

            def low(i, c):
                dve.wait_ge(high_ready, i + 1)
                for f in range(NF):
                    tokens = slice(512 * c, 512 * c + 512)
                    last = vec.tensor_tensor(feat_parts[:, 1, f, tokens], (pv, misc)[f][:, :], feat_parts[:, 0, f, tokens], ALU.subtract)
                last.then_inc(low_ready, 1)

            def routed(i, h):
                dve.wait_ge(silu_ready, routed_at(i, h + 1))
                vec.scalar_tensor_tensor(silu_h[:, h, :], st[h][:, 512:1024], 1.0 / W_SCALE, silu_h[:, h, :], ALU.mult, ALU.mult).then_inc(hidden_ready, 1)

            def take(i, c, t0, t1):
                if t0 == 0:
                    dve.wait_ge(y_done[c], (i - c) * 8 + 16)
                    apart(dve)
                for t in range(t0, t1):
                    dve.wait_ge(y_full, i * 4 + (t + 1))
                    vec.tensor_copy(tile_out[c][:, t, :], s1[t % 2][:, 0:D]).then_inc(y_free, 1)

            low(0, 0)
            low(1, 1)
            for h in range(2):
                routed(0, h)
            with dve.Fori(0, TILES // 2 - 1) as pair:
                for c in range(2):
                    i = pair * 2 + c
                    routed(i + 1, 0)
                    routed(i + 1, 1)
                    take(i, c, 0, 2)
                    low(i + 2, c)
                    take(i, c, 2, 4)
            for h in range(2):
                routed(TILES - 1, h)
            for c in range(2):
                take(TILES - 2 + c, c, 0, 4)

            def pick(b, c):
                vec.tensor_copy(slot_now[:, c, :, :].rearrange("p r t -> p (r t)"), slot_all[:, bass.ds(b, 1), :].rearrange("p o n -> p (o n)")).then_inc(pick_ready, 1)

            def add_experts(pair, c):
                b = pair * 2 + c
                dve.wait_ge(picked_in[c], pair * LISTED + LISTED)
                apart(dve)
                one, two = picked[c]
                steps = b * 3
                for t in range(NT):
                    last = vec.tensor_scalar(one[:, t, :], one[:, t, :], gate_all[:, bass.ds(b, 1), t], None, ALU.mult)
                last.then_inc(sum_step, 1)
                dve.wait_ge(sum_step, steps + 1)
                for t in range(NT):
                    last = vec.scalar_tensor_tensor(one[:, t, :], two[:, t, :], gate_all[:, bass.ds(b, 1), NT + t], one[:, t, :], ALU.mult, ALU.add)
                last.then_inc(sum_step, 1)
                dve.wait_ge(part_in[c], pair * 32 + 32)
                dve.wait_ge(sum_step, steps + 2)
                vec.tensor_tensor(one, one, part_g[c].unsqueeze(1).to_broadcast([P, NT, D]), ALU.mult).then_inc(sum_step, 1)
                dve.wait_ge(sum_step, steps + 3)
                vec.tensor_tensor(one, one, part_x[c], ALU.add).then_inc(sum_ready, 1)

            for c in range(2):
                pick(c, c)
            with dve.Fori(0, B // 2 - 1) as pair:
                for c in range(2):
                    add_experts(pair, c)
                    dve.wait_ge(sum_done[c], pair * 16 + 16)
                    pick(pair * 2 + (c + 2), c)
            for c in range(2):
                add_experts(B // 2 - 1, c)

        @block.tensor
        def _(pe):
            mm = nc.tensor.matmul
            pe.wait_ge(c_ready, 1)
            pe.wait_ge(pool_set, POOL_SET)
            for k in range(3):
                if k >= 2:
                    pe.wait_ge(s1_free, k - 1)
                for f in range(NF):
                    last = mm(s1[k % 2][0:B, :], silu_c[:, f, :], wmod_sb[:, f, k * 512:(k + 1) * 512], start=(f == 0), stop=(f == NF - 1))
                last.then_inc(s1_full, 1)
            pe.wait_ge(s1_free, 3)
            for i, idx in enumerate((0, 1, 3, 4)):
                for f in range(NF):
                    k = 2 * i + f
                    last = nc.tensor.transpose(s1[1][:, k * B:(k + 1) * B], mod_sb[:, idx * D + f * P:idx * D + (f + 1) * P], ident[0:B, 0:B])
            last.then_inc(s1_full, 1)

            def st_read(b, use):
                kind, i = use[0], use[1]
                if kind == "turn":
                    pe.wait_ge(feat1_ready, b * NF + (i + 1))
                elif kind == "qk":
                    pe.wait_ge(rest_ready, b * NG + (i + 1))
                elif kind == "v":
                    pe.wait_ge(v_ready, b * NT + (4 * i + 4))
                elif kind == "att":
                    pe.wait_ge(exp_done, b * STEPS * UNITS + (i * UNITS + use[2] + 1))
                elif kind == "ot":
                    pe.wait_ge(feat_ready, b * 3 * NF + (i + 1))
                elif kind == "op":
                    pe.wait_ge(scaled, b * 2 + (i + 1))
                elif kind == "ln":
                    pe.wait_ge(feat_ready, b * 3 * NF + (i + 2) * NF)
                else:
                    pe.wait_ge(hidden_ready, hidden_at(b, i, use[2] + 3))

            def st_use(b, head, use):
                i = ST_AT[head][use]
                if i >= 2:
                    old = ST_ORDER[head][i - 2]
                    st_read(b + 1 if old[0] in ("turn", "qk", "v") else b, old)
                else:
                    pe.wait_ge(hidden_ready, hidden_at(b, 0, i + 1))
                return st[i % 2]

            def head_use(b, use):
                if isinstance(b, int) and b == 0:
                    i = HEAD_USES.index(use)
                    if i >= 2:
                        st_read(0, HEAD_USES[i - 2])
                    return st[i % 2]
                return st_use(b - 1, True, use)

            def misc_use(b, name):
                before = MISC[MISC_AT[name] - 1]
                if name == MISC[0]:
                    pe.wait_ge(rows_ready, b * NG + HEAD_MAX)
                elif before == "router":
                    pe.wait_ge(score_ready, b + 1)
                elif before == "rank":
                    pe.wait_ge(slots_ready, b + 1)
                elif before.startswith("max"):
                    g = int(before[3:])
                    pe.wait_ge(rows_ready, b * NG + (g + 1 + (NG if g < HEAD_MAX else 0)))
                else:
                    pe.wait_ge(o_ready, b * STEPS + (int(before[3:]) + 1))

            def turn(to, src, f, ready, need):
                for t in range(NT):
                    pe.wait_ge(ready, need(t))
                    last = nc.tensor.transpose(to[:, t * P:(t + 1) * P], src[:, t, f * P:(f + 1) * P], ident[:, :])
                last.then_inc(st_full, 1)

            def turn1(b, f):
                turn(head_use(b, ("turn", f)), x1, f, norm1_ready, lambda t: b * NT + (t + 1))

            def qk(b, g):
                to = head_use(b, ("qk", g))
                pe.wait_ge(feat1_ready, b * NF + NF)
                for c in range(2):
                    for f in range(NF):
                        last = mm(to[:, c * 512:(c + 1) * 512], wqk_sb[:, g, f, :], feat1[:, f, c * 512:(c + 1) * 512],
                                  start=(f == 0), stop=(f == NF - 1))
                last.then_inc(st_full, 1)

            def make_v(b, h):
                to = head_use(b, ("v", h))
                for t in range(4):
                    for f in range(NF):
                        last = mm(to[:, t * D:(t + 1) * D], feat1[:, f, (4 * h + t) * P:(4 * h + t + 1) * P], wv_sb[:, f, :],
                                  start=(f == 0), stop=(f == NF - 1))
                last.then_inc(st_full, 1)

            def max_rows(g, i0, i1, at):
                for i in range(i0, i1):
                    j, (qt, k0, nk, _, _) = i // NM, MAXCH[i % NM]
                    pe.wait_ge(s1_free, at(i) - 1)
                    mm(s1[i % 2][:, 0:nk], q_stack[0:KS, g, j, qt * P:(qt + 1) * P], k_stack[0:KS, g, j, k0:k0 + nk],
                       start=True, stop=True).then_inc(s1_full, 1)

            def max_turn(b, g):
                pe.wait_ge(max_ready, b * NG + (g + 1))
                if g >= HEAD_MAX:
                    misc_use(b, f"max{g}")
                elif not isinstance(b, int) or b > 0:
                    misc_use(b - 1, f"max{g}")
                elif g >= 1:
                    pe.wait_ge(rows_ready, g)
                for qt in range(NT):
                    last = nc.tensor.transpose(misc_b[0:SHIFT * GH, qt * P:(qt + 1) * P],
                                               max_bf[:, qt, :, :].rearrange("p a j -> p (a j)"), ident_b[:, :])
                last.then_inc(misc_full, 1)

            def scores(b, head, n, u):
                g, c, j, t = n // NC, n % NC, u // 2, u % 2
                q0, nq, pieces, _ = CHUNKS[c]
                to = st_use(b, head, ("att", n, u))
                for kt, first, w, at in pieces:
                    if at // 1024 == t:
                        last = mm(to[:, at % 1024:at % 1024 + w], k_stack[0:KS + SHIFT, g, j, kt * P:(kt + 1) * P],
                                  q_stack[0:KS + SHIFT, g, j, q0 + first:q0 + nq], start=True, stop=True)
                last.then_inc(st_full, 1)

            def values(b, n, k0, k1):
                g, c = n // NC, n % NC
                _, nq, pieces, _ = CHUNKS[c]
                tiles = sorted(pieces)
                if k1 == k0:
                    return
                if k0 == 0:
                    pe.wait_ge(exp_done, b * STEPS * UNITS + (n + 1) * UNITS)
                    pe.wait_ge(masked, b * MASKS + sum(len(DIAG[i % NC]) * GH for i in range(n + 1)))
                    pe.wait_ge(raw_ready, b * STEPS + (n + 1))
                for kt, first, w, at in tiles[k0:k1]:
                    for j in range(GH):
                        h = (g * GH + j) * VW
                        last = mm(pv[32 * j:32 * j + 32, first:nq], v_sb[:, kt, h:h + 32],
                                  probs[:, n % 2, j * PTW + at:j * PTW + at + w], start=(kt == 0), stop=(kt == len(tiles) - 1))
                if k1 >= len(tiles):
                    last.then_inc(pv_full, 1)

            def turn_out(b, n):
                nq = CHUNKS[n % NC][1]
                pe.wait_ge(raw_ready, b * STEPS + (n + 2))
                misc_use(b, f"out{n}")
                for t in range(nq // P):
                    last = nc.tensor.transpose(misc[:, t * P:(t + 1) * P], o_raw[:, t * P:(t + 1) * P], ident[:, :])
                last.then_inc(misc_full, 1)

            def up_half(to, s, c, h, between=None, done=st_full):
                for m in range(2):
                    for i in range(len(W_PART)):
                        for f in range(NF):
                            last = mm(to[:, 512 * m:512 * m + 512], w_up[s][W_PART[i]][:, f, m * RH + h * P:m * RH + (h + 1) * P],
                                      feat_parts[:, A_PART[i], f, c * 512:(c + 1) * 512],
                                      start=(i == 0 and f == 0), stop=(i == len(W_PART) - 1 and f == NF - 1))
                        if m == 1 and i == len(W_PART) - 1:
                            last.then_inc(done, 1)
                        if between:
                            between((h * 2 + m) * len(W_PART) + i)

            def out_tile(to, s, c, t):
                for i in range(len(W_PART)):
                    for h in range(2):
                        last = mm(to[:, 0:D], hidden[:, c, A_PART[i], h, t * P:(t + 1) * P], w_down[s][W_PART[i]][:, h, :],
                                  start=(i == 0 and h == 0), stop=(i == len(W_PART) - 1 and h == 1))
                return last

            def down(b, u, c, s, at):
                pe.wait_ge(hidden_low, hidden_at(b, u, 2 * c + 4))
                for t in range(4):
                    pe.wait_ge(s1_free, at(t) - 1)
                    out_tile(s1[t % 2], s, c, t).then_inc(s1_full, 1)

            def batch(b, head):
                pe.wait_ge(v_ready, (b + 1) * NT)
                for n in range(STEPS):
                    g, c = n // NC, n % NC
                    ahead = 0
                    if c == 0:
                        if n >= 1:
                            ahead = len(CHUNKS[NC - 1][2]) * 2 // 3
                            values(b, n - 1, 0, ahead)
                        pe.wait_ge(shift_in, (b * NG + (g + 1)) * 16)
                    for i, (n0, _) in STEP_MAX.items():
                        if n == n0:
                            pe.wait_ge(stacked[i], (b + 1) * STACK)
                    for u in range(UNITS):
                        scores(b, head, n, u)
                        if u == 1 and n >= 2:
                            turn_out(b, n - 2)
                        for i in range(3):
                            to, i0, i1 = step_max(n, u, i)
                            max_rows(to, i0, i1, lambda i: s1_at(b, head, ("max", to, i)))
                            if u >= 2 and n >= 1:
                                k, x = len(CHUNKS[(n - 1) % NC][2]) - ahead, 3 * (u - 2) + i
                                values(b, n - 1, ahead + k * x // 18, ahead + k * (x + 1) // 18)
                    for i, (_, n1) in STEP_MAX.items():
                        if n == n1 - 1:
                            max_turn(b, i)
                values(b, STEPS - 1, 0, NT)
                turn_out(b, STEPS - 2)
                turn_out(b, STEPS - 1)
                for f in range(NF):
                    turn(st_use(b, head, ("ot", f)), o_tok, f, o_ready, lambda t: (b + 1) * STEPS)
                pe.wait_ge(feat_ready, b * 3 * NF + NF)
                for h in range(2):
                    to = st_use(b, head, ("op", h))
                    for t in range(4):
                        for f in range(NF):
                            last = mm(to[:, t * D:(t + 1) * D], feat[:, f, (4 * h + t) * P:(4 * h + t + 1) * P], wo_sb[:, f, :],
                                      start=(f == 0), stop=(f == NF - 1))
                    last.then_inc(st_full, 1)

                def turn2(h):
                    to = st_use(b, head, ("ln", h))
                    for t in range(4):
                        pe.wait_ge(norm2_ready, b * NT + (4 * h + t + 1))
                        for f in range(NF):
                            last = nc.tensor.transpose(to[:, f * 512 + t * P:f * 512 + (t + 1) * P],
                                                       norm[:, 4 * h + t, f * P:(f + 1) * P], ident[:, :])
                    last.then_inc(st_full, 1)

                turn2(0)
                for kind, *at in moves(head):
                    if kind == "up":
                        u, c, g, i0, i1 = at
                        if i1 > i0 and i0 == 0:
                            pe.wait_ge(stacked[g], (b + 2) * STACK)

                        def between(x):
                            if u + c + i1 == 0 and x == len(W_PART) - 1:
                                turn2(1)
                            max_rows(g, i0 + (i1 - i0) * x // 12, i0 + (i1 - i0) * (x + 1) // 12, lambda i: head_max(b + 1, g, i))

                        if c == 0:
                            pe.wait_ge(ffn_in[u % 2], b * (NS // 2 * 16) + (u // 2 + 1) * 16)
                        if u == 0:
                            pe.wait_ge(feat_low, b * 2 + (c + 1))
                        for h in range(2):
                            up_half(st_use(b, head, ("ffn", u, 2 * c + h)), u % 2, c, h, between)
                    elif kind == "down":
                        down(b, *at, at[0] % 2, lambda t: s1_at(b, head, ("down", *at, t)))
                        if at == [1, 1] and not head:
                            misc_use(b, "max0")
                            mm(misc[:, 0:NE], ones[:, :], before[:, NT, :], start=True, stop=True).then_inc(misc_full, 1)
                    elif kind == "router":
                        misc_use(b, "router")
                        for t in range(NT):
                            if t % 4 == 0:
                                pe.wait_ge(feat_ready, b * 3 * NF + (t // 4 + 2) * NF)
                            for f in range(NF):
                                last = mm(misc[:, t * NE:(t + 1) * NE], feat[:, f, t * P:(t + 1) * P], rw_sb[:, f, :], start=(f == 0), stop=(f == NF - 1))
                        last.then_inc(misc_full, 1)
                    elif kind == "rank":
                        misc_use(b, "rank")
                        pe.wait_ge(chosen_ready, b + 1)
                        mm(misc[:, 0:NT * NE], tri[:, :], chosen[:, :, :].rearrange("p t e -> p (t e)"), start=True, stop=False)
                        mm(misc[:, 0:NT * NE], ones[:, :], before[:, 0:NT, :].rearrange("p t e -> p (t e)"), start=False, stop=True).then_inc(misc_full, 1)
                    elif kind == "turn":
                        turn1(b + 1, at[0])
                    elif kind == "qk":
                        qk(b + 1, at[0])
                    elif kind == "v":
                        make_v(b + 1, at[0])
                    elif kind == "max_turn":
                        max_turn(b + 1, at[0])

            for f in range(NF):
                turn1(0, f)
            for g in range(NG):
                qk(0, g)
            for h in range(2):
                make_v(0, h)
            for g in range(HEAD_MAX):
                pe.wait_ge(stacked[g], STACK)
                max_rows(g, 0, MAX0, lambda i: head_max(0, g, i))
                max_turn(0, g)
            with pe.Fori(0, B - 1) as b:
                batch(b, True)
            batch(B - 1, False)

            def turn_rows(i, c, first=False):
                pe.wait_ge(rows_in[c], (i - c) * 8 + 16)
                if not first:
                    pe.wait_ge(low_ready, i)
                for f in range(NF):
                    for t in range(4):
                        last = nc.tensor.transpose((pv, misc)[f][:, t * P:(t + 1) * P], tile_in[c][:, t, f * P:(f + 1) * P], ident[:, :])
                last.then_inc(turned, 1)

            def routed_up(i, s, weights):
                pe.wait_ge(w_in[s], weights)
                pe.wait_ge(low_ready, i + 1)
                for h in range(2):
                    pe.wait_ge(hidden_ready, routed_at(i, h + 1))
                    up_half(st[h], s, s % 2, h, done=up_full)

            def routed_down(i, s):
                pe.wait_ge(hidden_low, routed_at(i, 4))
                for t in range(4):
                    pe.wait_ge(y_free, i * 4 + (t + 1))
                    out_tile(s1[t % 2], s, s % 2, t).then_inc(y_full, 1)

            pe.wait_ge(table_ready, 1)
            turn_rows(0, 0, True)
            turn_rows(1, 1)
            routed_up(0, 0, 16)
            with pe.Fori(0, TILES // WSLOTS - 1) as quad:
                for s in range(WSLOTS):
                    i, to = quad * WSLOTS + s, (s + 1) % WSLOTS
                    routed_up(i + 1, to, quad * 16 + (16 if to else 32))
                    turn_rows(i + 2, s % 2)
                    routed_down(i, s)
            for i in range(TILES - WSLOTS, TILES):
                s = i % WSLOTS
                if i + 1 < TILES:
                    routed_up(i + 1, s + 1, TILES // WSLOTS * 16)
                if i + 2 < TILES:
                    turn_rows(i + 2, s % 2)
                routed_down(i, s)


def kernel(**inputs):
    import numpy as np
    import concourse.bacc as bacc
    from concourse.bass_utils import run_bass_kernel_spmd

    a = {n[3:]: np.asarray(v) for n, v in inputs.items()}
    tight = np.ascontiguousarray
    qkv = a["attn_w_qkv"].reshape(NF, P, NG, GH, 3, HD)
    w_qk = tight(qkv[:, :, :, :, 0:2].transpose(1, 2, 0, 4, 5, 3)).reshape(P, NG, NF, P)
    w_v = tight(qkv[:, :, :, :, 2].transpose(1, 0, 2, 3, 4)).reshape(P, NF, D)
    w_o = tight(a["attn_w_o"].reshape(NF, P, D).transpose(1, 0, 2))

    def unit(w1, w2, w3):
        w_up = np.concatenate([w1, w2], 0).reshape(2 * RH, NF, P).transpose(2, 1, 0).reshape(P, -1)
        w_down = w3.reshape(D, 2, P).transpose(2, 1, 0).reshape(P, -1)
        return np.concatenate([w_up, w_down], 1)

    units = [unit(a["ffn_shared_w1"][h:h + RH], a["ffn_shared_w2"][h:h + RH], a["ffn_shared_w3"][:, h:h + RH]) for h in range(0, SH, RH)]
    units += [unit(a["ffn_w12"][e, :RH], a["ffn_w12"][e, RH:], a["ffn_w3"][e]) for e in range(NE)]
    arrays = {
        "x": tight(a["attn_x"]),
        "w_qk": w_qk, "w_v": w_v, "w_o": w_o,
        "ffn_w": tight(np.stack(units)),
        "router_w": tight(a["ffn_router_w"].reshape(NE, NF, P).transpose(2, 1, 0)),
        "bias": tight(np.broadcast_to(a["ffn_expert_bias"], (P, NE))),
        "c_t": tight(a["c"].reshape(B, NF, P).transpose(2, 1, 0)).reshape(P, NF * B),
        "w_mod": tight(a["wmod"].reshape(NF, P, 6 * D).transpose(1, 0, 2)),
    }
    nc = bacc.Bacc("TRN2", target_bir_lowering=False, num_devices=1)
    args = {n: nc.dram_tensor(n, v.shape, mybir.dt.from_np(v.dtype), kind="ExternalInput").ap() for n, v in arrays.items()}
    args["out"] = nc.dram_tensor("out", (B, T, D), F32, kind="ExternalOutput").ap()
    adaln_layer(nc, **args)
    r = run_bass_kernel_spmd(nc, [arrays], core_ids=[0])
    return r.results[0]["out"]
```
